# Optimizing a Trainium2 kernel written in Bass

```python
import numpy as np
import jax
import jax.numpy as jnp

def _softmax(x, axis=-1):
    return jax.nn.softmax(x, axis=axis)

def _gelu(x):
    return jax.nn.gelu(x, approximate=True)

def _silu(x):
    return jax.nn.silu(x)

def _sigmoid(x):
    return jax.nn.sigmoid(x)

def _layernorm(x, axis=-1, eps=1e-05):
    m = jnp.mean(x, axis=axis, keepdims=True)
    v = jnp.var(x, axis=axis, keepdims=True)
    return (x - m) / jnp.sqrt(v + eps)

def _scatter_add(tgt, idx, src, axis=0):
    return tgt.at[idx].add(src)

def _segment_sum(src, seg, n):
    return jax.ops.segment_sum(src, seg, n)
kernel_name = 'mk_sandwich_d1_jaxref_r8_e0248d'

def setup_inputs(seed: int=0):
    np.random.seed(seed)
    _w = jnp.asarray

    def _L0_attn_setup():
        import jax, jax.numpy as jnp
        import numpy as np
        B, T, C = (4, 512, 128)
        key = jax.random.key(seed)
        ks = jax.random.split(key, 6)
        s = 1.0 / np.sqrt(C)
        x = jax.random.normal(ks[0], (B, T, C), dtype=jnp.float32)
        Wi = jax.random.uniform(ks[1], (C, C), jnp.float32, -s, s)
        bi = jax.random.uniform(ks[2], (C,), jnp.float32, -s, s)
        Wr = jax.random.uniform(ks[3], (C, C), jnp.float32, -s, s)
        br = jax.random.uniform(ks[4], (C,), jnp.float32, -s, s)
        cap_lambda = jax.random.uniform(ks[5], (1,), jnp.float32, 0.9, 0.999)
        return {'x': x, 'Wi': Wi, 'bi': bi, 'Wr': Wr, 'br': br, 'cap_lambda': cap_lambda}
    _L0_attn_in = _L0_attn_setup()

    def _L0_ffn_setup():
        import jax, jax.numpy as jnp
        import numpy as np
        E = 32
        K = 4
        H = 128
        I = 96
        ROUTED_SCALING_FACTOR = 1.0
        key = jax.random.key(seed)
        k0, k1, k2, k3, k4, k5 = jax.random.split(key, 6)
        return {'hidden_states': jax.random.normal(k0, (1, 256, H), jnp.float32), 'gate_w': jax.random.normal(k1, (E, H), jnp.float32) * 0.02, 'w1': jax.random.normal(k2, (E, H, I), jnp.float32) * 0.02, 'w3': jax.random.normal(k3, (E, H, I), jnp.float32) * 0.02, 'w2': jax.random.normal(k4, (E, I, H), jnp.float32) * 0.02, 'e_bias': jax.random.normal(k5, (E,), jnp.float32) * 0.02}
    _L0_ffn_in = _L0_ffn_setup()
    _d = {'L0_attn_x': _L0_attn_in['x'], 'L0_attn_Wi': _L0_attn_in['Wi'], 'L0_attn_bi': _L0_attn_in['bi'], 'L0_attn_Wr': _L0_attn_in['Wr'], 'L0_attn_br': _L0_attn_in['br'], 'L0_attn_cap_lambda': _L0_attn_in['cap_lambda'], 'L0_ffn_gate_w': _L0_ffn_in['gate_w'], 'L0_ffn_w1': _L0_ffn_in['w1'], 'L0_ffn_w3': _L0_ffn_in['w3'], 'L0_ffn_w2': _L0_ffn_in['w2'], 'L0_ffn_e_bias': _L0_ffn_in['e_bias']}
    _x0 = _d['L0_attn_x']
    _d['L0_attn_x'] = jax.random.normal(jax.random.fold_in(jax.random.key(seed), 1), (16, 256, 128), dtype=_x0.dtype)
    del _x0
    return _d

def reference(L0_attn_x, L0_attn_Wi, L0_attn_bi, L0_attn_Wr, L0_attn_br, L0_attn_cap_lambda, L0_ffn_gate_w, L0_ffn_w1, L0_ffn_w3, L0_ffn_w2, L0_ffn_e_bias):

    def _L0_attn_ref(x, Wi, bi, Wr, br, cap_lambda):
        import jax, jax.numpy as jnp
        import numpy as np
        B, T, C = (4, 512, 128)
        it = jax.nn.sigmoid(jnp.einsum('btc,dc->btd', x, Wi) + bi)
        rt = jax.nn.sigmoid(jnp.einsum('btc,dc->btd', x, Wr) + br)
        at = jnp.exp(-8.0 * jax.nn.softplus(cap_lambda) * rt)
        gx = jnp.sqrt(1.0 - at ** 2) * (it * x)

        def step(h, inp):
            a, g = inp
            h = a * h + g
            return (h, h)
        _, ys = jax.lax.scan(step, jnp.zeros((x.shape[0], x.shape[2]), x.dtype), (jnp.swapaxes(at, 0, 1), jnp.swapaxes(gx, 0, 1)))
        return jnp.swapaxes(ys, 0, 1)

    def _L0_ffn_ref(hidden_states, gate_w, w1, w3, w2, e_bias):
        import jax, jax.numpy as jnp
        import numpy as np
        E = 32
        K = 4
        H = 128
        I = 96
        ROUTED_SCALING_FACTOR = 1.0
        orig_shape = hidden_states.shape
        x = hidden_states.reshape(-1, orig_shape[-1])
        T = x.shape[0]
        router_logits = x @ gate_w.T
        scores = jax.nn.sigmoid(router_logits.astype(jnp.float32))
        _, topk_ids = jax.lax.top_k(scores + e_bias[None, :], K)
        topk_w = jnp.take_along_axis(scores, topk_ids, axis=1)
        topk_w = topk_w / jnp.sum(topk_w, axis=1, keepdims=True)
        combine = jnp.zeros((T, E), jnp.float32).at[jnp.arange(T)[:, None], topk_ids].add(topk_w)
        g = jnp.einsum('th,ehi->tei', x, w1)
        u = jnp.einsum('th,ehi->tei', x, w3)
        a = jax.nn.silu(g) * u * combine[:, :, None].astype(x.dtype)
        out = jnp.einsum('tei,eih->th', a, w2)
        out = out * ROUTED_SCALING_FACTOR
        return out.reshape(orig_shape)
    x = L0_attn_x
    x = x + _layernorm(_L0_attn_ref(_layernorm(x, axis=-1), L0_attn_Wi, L0_attn_bi, L0_attn_Wr, L0_attn_br, L0_attn_cap_lambda), axis=-1)
    x = x + _layernorm(_L0_ffn_ref(_layernorm(x, axis=-1), L0_ffn_gate_w, L0_ffn_w1, L0_ffn_w3, L0_ffn_w2, L0_ffn_e_bias), axis=-1)
    return x

_drawn_inputs = setup_inputs


def setup_inputs(seed=0):
    import zlib

    import numpy as np

    out = dict(_drawn_inputs(seed))
    spreads = {}
    factors = {'L0_attn_br': 4.451}
    for name, (base, spread) in spreads.items():
        noise = np.random.default_rng([zlib.crc32(name.encode()), seed]).standard_normal(out[name].shape)
        drawn = base * np.exp(spread * noise) if base else spread * noise
        out[name] = jnp.asarray(drawn.astype(out[name].dtype))
    for name, factor in factors.items():
        out[name] = (out[name] * factor).astype(out[name].dtype)
    return out
```

```python
from contextlib import ExitStack

import concourse.bass as bass
from concourse import mybir

ALU = mybir.AluOpType
ACT = mybir.ActivationFunctionType
AX_X = mybir.AxisListType.X
F32 = mybir.dt.float32
BF16 = mybir.dt.bfloat16
U32 = mybir.dt.uint32
I32 = mybir.dt.int32

P = 128
EPS = 1e-5
K = 4
GT = 4
HALVES = 2
SLOTS = 4
DVE_TABLES = 26
DVE_ROUTE = 15


def sandwich_kernel(nc: bass.Bass, x, Wi, bi, Wr, br, cap, gate_w, w1, w3, w2, e_bias, out, xs, ys):
    B, T, C = x.shape
    E, _, I = w1.shape
    TILES = B * T // P
    G = TILES // GT
    GH = G // HALVES
    TH = TILES // HALVES
    GC = GT * P
    SEQ = T
    REGION = TH * P + P
    MAX_BLOCKS = ys[0].shape[0] // P
    assert C == P and GC % SEQ == 0

    x_rows = x.rearrange("b t c -> (b t) c").rearrange("(n p) c -> p n c", p=P)
    out_rows = out.rearrange("b t c -> (b t) c").rearrange("(n p) c -> p n c", p=P)

    with ExitStack() as ctx:
        def sb(name, shape, dt=F32):
            return ctx.enter_context(nc.sbuf_tensor(name, shape, dt))

        def sem(name):
            return ctx.enter_context(nc.semaphore(name))

        bank = [ctx.enter_context(nc.psum_tensor(f"bank{i}", [P, 512], F32)) for i in range(8)]
        ps_xnT, ps_zi, ps_zr, ps_h, ps_x2T, ps_logit, ps_pos = bank[:7]
        ps_setup = bank[7]
        ps_xbT, ps_gu, ps_aT, ps_y = (bank[2 * i:2 * i + 2] for i in range(4))

        wi_raw, wr_raw, gate_raw = sb("wi_raw", [P, C]), sb("wr_raw", [P, C]), sb("gate_raw", [E, C])
        wiT, wrT, gateT = sb("wiT", [C, P]), sb("wrT", [C, P]), sb("gateT", [C, E])
        w13_sb = sb("w13_sb", [C, E, 2, I])
        w2_sb = sb("w2_sb", [I, E, C])
        bias_i, bias_r, decay = sb("bias_i", [P, 1]), sb("bias_r", [P, 1]), sb("decay", [P, 6])
        ebias = sb("ebias", [P, E])
        ident = sb("ident", [P, P])
        before = sb("before", [P, P], BF16)
        ones = sb("ones", [P, P], BF16)
        iota_e, region_e, iota_p = sb("iota_e", [P, E]), sb("region_e", [P, E]), sb("iota_p", [P, 1])
        iota_row = sb("iota_row", [1, E])
        eps_c, neg_half = sb("eps_c", [P, 1]), sb("neg_half", [P, GT])
        zeros = sb("zeros", [P, P])

        x_sb = sb("x_sb", [P, TILES, C])
        xn2_all = sb("xn2_all", [P, TILES, C])
        row_xs, row_ys = sb("row_xs", [P, TILES * K], U32), sb("row_ys", [P, TILES * K], U32)
        row_f = sb("row_f", [P, TILES, K])
        wt_all = sb("wt_all", [P, TILES, K])

        st1, mv1, std1 = sb("st1", [P, GT, 6]), sb("mv1", [P, GT, 2]), sb("std1", [P, GT])
        rstd1, xn, xnT = sb("rstd1", [P, GT]), sb("xn", [P, GT, C]), sb("xnT", [C, GC])
        ti, tr, at, at2, bq = (sb(n, [P, GC]) for n in ("ti", "tr", "at", "at2", "bq"))
        gated, gx, hT = sb("gated", [P, GC]), sb("gx", [P, GC]), sb("hT", [P, GC])
        sth, mvh, stdh = sb("sth", [P, GT, 6]), sb("mvh", [P, GT, 2]), sb("stdh", [P, GT])
        rstdh, hn = sb("rstdh", [P, GT]), sb("hn", [P, GT, C])
        st2, mv2, std2 = sb("st2", [P, GT, 6]), sb("mv2", [P, GT, 2]), sb("std2", [P, GT])
        rstd2, xn2, xn2T = sb("rstd2", [P, GT]), sb("xn2", [P, GT, C]), sb("xn2T", [C, GC])
        th, score, biased = sb("th", [P, GT, E]), sb("score", [P, GT, E]), sb("biased", [P, GT, E])
        top, top_i, top_f = sb("top", [P, GT, 8]), sb("top_i", [P, GT, 8], U32), sb("top_f", [P, GT, K])
        hot_all, picked = sb("hot_all", [P, TILES, K, E], BF16), sb("picked", [P, GT, K, E])
        mask, seen, add4 = sb("mask", [P, GT, E], BF16), sb("seen", [P, E], BF16), sb("add4", [P, E])
        pos = sb("pos", [P, GT, E])
        wsel, wsum, winv = sb("wsel", [P, GT, K]), sb("wsum", [P, GT]), sb("winv", [P, GT])

        cnt, cnt_up, nblk_i, nblk = sb("cnt", [P, E]), sb("cnt_up", [P, E], I32), sb("nblk_i", [P, E], I32), sb("nblk", [P, E])
        pack = sb("pack", [P, E])
        cum, past, past_n = sb("cum", [P, E]), sb("past", [P, E]), sb("past_n", [P, E])
        ones_e = sb("ones_e", [P, E])
        tcol = sb("tcol", [P, 8])
        steps_f, steps_u = sb("steps_f", [1, 2]), sb("steps_u", [1, 2], I32)
        expert_of = [sb(f"expert_of{h}", [1, P], I32) for h in range(HALVES)]
        row_of = [sb(f"row_of{h}", [1, P], I32) for h in range(HALVES)]
        tail_of = [sb(f"tail_of{h}", [1, E], I32) for h in range(HALVES)]
        steps_of = [sb(f"steps_of{h}", [1, 1], I32) for h in range(HALVES)]

        xb = sb("xb", [P, SLOTS, C])
        xbT, act_t = sb("xbT", [C, 2, 2, P]), sb("act_t", [P, 2, 2, I])
        silu2, act_a = sb("silu2", [P, 2, 2, I]), sb("act_a", [P, 2, 2, I])
        aT, yb = sb("aT", [I, 2, 2, P]), sb("yb", [P, SLOTS, C])

        yk = [sb(f"yk{h}", [P, TH, K, C]) for h in range(HALVES)]
        mix = sb("mix", [P, 2, GT, C])
        st3, mv3, ve3, rstd3 = sb("st3", [P, GT, 6]), sb("mv3", [P, 2, GT, 2]), sb("ve3", [P, 2, GT]), sb("rstd3", [P, 2, GT])
        fin = sb("fin", [P, 2, GT, C])

        s_wmix, s_wexp, s_small, s_x = sem("s_wmix"), sem("s_wexp"), sem("s_small"), sem("s_x")
        s_const, s_z0, s_setT, s_wT, s_bias, s_decay = (sem(n) for n in (
            "s_const", "s_z0", "s_setT", "s_wT", "s_bias", "s_decay"))
        v_var1, a_std1, v_xn, pe_xnT, a_xnT, pe_z, a_at, a_gate, v_gated, v_scan, pe_h = (sem(n) for n in (
            "v_var1", "a_std1", "v_xn", "pe_xnT", "a_xnT", "pe_z", "a_at", "a_gate", "v_gated", "v_scan", "pe_h"))
        v_varh, a_stdh, v_x1, v_var2, a_std2 = (sem(n) for n in ("v_varh", "a_stdh", "v_x1", "v_var2", "a_std2"))
        v_xn2, pe_x2T, a_x2T, a_x2c, pe_logit, a_th, v_mask, pe_pos, v_row, v_wt, v_seen = (sem(n) for n in (
            "v_xn2", "pe_x2T", "a_x2T", "a_x2c", "pe_logit", "a_th", "v_mask", "pe_pos", "v_row", "v_wt", "v_seen"))
        l_ln1, l_scan, l_x1, l_route, l_act, l_tab, l_mix = (sem(n) for n in (
            "l_ln1", "l_scan", "l_x1", "l_route", "l_act", "l_tab", "l_mix"))
        s_scat = [sem(f"s_scat{h}") for h in range(HALVES)]
        v_pack = sem("v_pack")
        pe_cnt, v_tcol, pe_tab, v_tab = sem("pe_cnt"), sem("v_tcol"), sem("pe_tab"), sem("v_tab")
        s_fill = [sem(f"s_fill{h}") for h in range(HALVES)]
        s_tail = [sem(f"s_tail{h}") for h in range(HALVES)]
        s_xb = [[sem(f"s_xb{h}_{u}") for u in range(SLOTS)] for h in range(HALVES)]
        s_ys = [[sem(f"s_ys{h}_{u}") for u in range(SLOTS)] for h in range(HALVES)]
        b_xT, b_xTc, b_gu, b_tanh, b_silu, b_act, b_aT, b_aTc, b_y, b_yc = (
            [sem(f"{n}{h}") for h in range(HALVES)] for n in (
                "b_xT", "b_xTc", "b_gu", "b_tanh", "b_silu", "b_act", "b_aT", "b_aTc", "b_y", "b_yc"))
        s_yk = [sem("s_yk0"), sem("s_yk1")]
        c_ve, c_pow, s_fin, c_fin = sem("c_ve"), sem("c_pow"), sem("s_fin"), sem("c_fin")
        s_out = [sem("s_out0"), sem("s_out1")]

        def ge(eng, s, n):
            if not isinstance(n, int) or n > 0:
                eng.wait_ge(s, n)

        def wait_apart(eng, s, n):
            if not isinstance(n, int):
                eng.to_reg(n)
            eng.wait_ge(s_const, 2)
            eng.wait_ge(s, n)

        def steps_value(eng, h):
            eng.wait_ge(v_tab, h + 1)
            return eng.value_load(steps_of[h][0:1, 0:1], min_val=TH * K // SLOTS, max_val=MAX_BLOCKS // SLOTS)

        block = ctx.enter_context(nc.Block())

        @block.sync
        def _(sp):
            sp.dma_start(x_sb[:, 0:GT, :], x_rows[:, 0:GT, :]).then_inc(s_x, 16)
            sp.dma_start(wi_raw[:], Wi).then_inc(s_wmix, 16)
            sp.dma_start(wr_raw[:], Wr).then_inc(s_wmix, 16)
            sp.dma_start(gate_raw[:], gate_w).then_inc(s_wmix, 16)
            with nc.allow_non_contiguous_dma(reason="one bias per channel"):
                sp.dma_start(bias_i[:], bi.rearrange("(p a) -> p a", a=1)).then_inc(s_small, 16)
                sp.dma_start(bias_r[:], br.rearrange("(p a) -> p a", a=1)).then_inc(s_small, 16)
                sp.dma_start(decay[:, 0:1], cap.rearrange("(a b) -> a b", a=1).to_broadcast([P, 1])).then_inc(s_small, 16)
                sp.dma_start(ebias[:], e_bias.rearrange("(a b) -> a b", a=1).to_broadcast([P, E])).then_inc(s_small, 16)
            for g in range(1, G):
                sp.wait_ge(s_x, 16 * g)
                sp.dma_start(x_sb[:, g * GT:(g + 1) * GT, :], x_rows[:, g * GT:(g + 1) * GT, :]).then_inc(s_x, 16)
            sp.dma_start(w13_sb[:, :, 0, :], w1.rearrange("e h i -> h e i")).then_inc(s_wexp, 16)
            sp.dma_start(w13_sb[:, :, 1, :], w3.rearrange("e h i -> h e i")).then_inc(s_wexp, 16)
            sp.dma_start(w2_sb[:], w2.rearrange("e i h -> i e h")).then_inc(s_wexp, 16)
            sp.wait_ge(s_const, 2)
            for h in range(HALVES):
                sp.dma_start(ys[h].rearrange("(n p) c -> p n c", p=P)[:, TH * K:, :],
                             zeros[:].unsqueeze(1).to_broadcast([P, MAX_BLOCKS - TH * K, C])).then_inc(s_fill[h], 16)
                for u in range(SLOTS):
                    r = E * REGION + u * P
                    sp.dma_start(xs[h][r:r + P, :], zeros[:]).then_inc(s_ys[h][u], 16)
            for h in range(HALVES):
                sp.wait_ge(v_tab, h + 1)
                with sp.Fori(0, E) as e:
                    r = sp.value_load(tail_of[h][0:1, bass.ds(e, 1)], min_val=0, max_val=E * REGION - P)
                    sp.dma_start(xs[h][bass.ds(r, P), :], zeros[:]).then_inc(s_tail[h], 16)
            for h in range(HALVES):
                sp.wait_ge(s_tail[h], 16 * E)
                sp.wait_ge(s_fill[h], 16)
                for u in range(SLOTS):
                    sp.wait_ge(s_ys[h][u], 16)
                sp.wait_ge(s_scat[h], 16 * TH * K)
                steps = steps_value(sp, h)

                def rows(q, u):
                    return sp.value_load(row_of[h][0:1, bass.ds(q * SLOTS + u, 1)], min_val=0, max_val=(E + 1) * REGION - P)

                def load(r, u):
                    sp.dma_start(xb[:, u, :], xs[h][bass.ds(r, P), :]).then_inc(s_xb[h][u], 16)

                def store(q, u):
                    sp.dma_start(ys[h][bass.ds((q * SLOTS + u) * P, P), :], yb[:, u, :]).then_inc(s_ys[h][u], 16)

                if h:
                    wait_apart(sp, b_xT[h - 1], steps_value(sp, h - 1) * SLOTS)
                for u in range(SLOTS):
                    load(rows(0, u), u)
                with sp.Fori(0, steps - 1) as q:
                    for u in range(SLOTS):
                        r = rows(q + 1, u)
                        sp.wait_ge(b_xT[h], q * SLOTS + u + 1)
                        load(r, u)
                    for u in range(SLOTS):
                        sp.wait_ge(b_yc[h], q * 2 + u // 2 + 1)
                        store(q, u)
                sp.wait_ge(b_yc[h], steps * 2)
                for u in range(SLOTS):
                    store(steps - 1, u)
            for h in range(HALVES):
                for g in range(h * GH, h * GH + GH):
                    sp.wait_ge(c_fin, g + 1)
                    sp.dma_start(out_rows[:, g * GT:(g + 1) * GT, :], fin[:, g % 2, :, :]).then_inc(s_out[g % 2], 16)
            for p in range(2):
                sp.wait_ge(s_out[p], 16 * G // 2)

        @block.gpsimd
        def _(pool):
            pool.memset(zeros[:], 0.0).then_inc(s_const, 1)
            pool.memset(ident[:], 0.0).then_inc(s_z0, 1)
            pool.memset(before[:], 1.0).then_inc(s_z0, 1)
            pool.memset(ones[:], 1.0)
            pool.memset(eps_c[:], EPS)
            pool.memset(neg_half[:], -0.5)
            pool.memset(ones_e[:], 1.0)
            pool.memset(seen[:], 0.0)
            pool.iota(iota_e[:], pattern=[[1, E]], base=0, channel_multiplier=0, allow_small_or_imprecise_dtypes=True)
            pool.iota(region_e[:], pattern=[[REGION, E]], base=0, channel_multiplier=0, allow_small_or_imprecise_dtypes=True)
            pool.iota(iota_p[:], pattern=[[0, 1]], base=0, channel_multiplier=1, allow_small_or_imprecise_dtypes=True)
            pool.wait_ge(s_z0, 2)
            pool.affine_select(out=ident[:], in_=ident[:], compare_op=ALU.not_equal, fill=1.0, base=0,
                               pattern=[[-1, P]], channel_multiplier=1)
            pool.affine_select(out=before[:], in_=before[:], compare_op=ALU.is_ge, fill=0.0, base=-1,
                               pattern=[[1, P]], channel_multiplier=-1).then_inc(s_const, 1)
            for h in range(HALVES):
                for g in range(h * GH, h * GH + GH):
                    pool.wait_ge(v_row, g + 1)
                    pool.wait_ge(a_x2c, g + 1)
                    for j in range(GT):
                        for k in range(K):
                            pool.indirect_dma_start(
                                out=xs[h], out_offset=bass.IndirectOffsetOnAxis(
                                    ap=row_xs[:, (g * GT + j) * K + k:(g * GT + j) * K + k + 1], axis=0),
                                in_=xn2_all[:, g * GT + j, :],
                                in_offset=None).then_inc(s_scat[h], 16)
            for h in range(HALVES):
                steps = steps_value(pool, h)
                for u in range(SLOTS):
                    wait_apart(pool, s_ys[h][u], steps * 16 + 16)
                pool.wait_ge(v_pack, (h + 1) * GH)
                for g in range(h * GH, h * GH + GH):
                    for j in range(GT):
                        for k in range(K):
                            pool.indirect_dma_start(
                                out=yk[h][:, g * GT + j - h * TH, k, :], out_offset=None, in_=ys[h],
                                in_offset=bass.IndirectOffsetOnAxis(ap=row_ys[:, (g * GT + j) * K + k:(g * GT + j) * K + k + 1], axis=0),
                            ).then_inc(s_yk[g % 2], 16)
                    if g == G - 1:
                        for p in (g - 1, g):
                            pool.wait_ge(c_ve, p + 1)
                            pool.tensor_tensor(out=rstd3[:, p % 2, :], in0=ve3[:, p % 2, :], in1=neg_half[:],
                                               op=ALU.pow).then_inc(c_pow, 1)
                    elif g:
                        pool.wait_ge(c_ve, g)
                        pool.tensor_tensor(out=rstd3[:, (g - 1) % 2, :], in0=ve3[:, (g - 1) % 2, :], in1=neg_half[:],
                                           op=ALU.pow).then_inc(c_pow, 1)

        @block.scalar
        def _(act):
            act.wait_ge(s_small, 64)
            act.activation(decay[:, 1:2], decay[:, 0:1], ACT.Abs).then_inc(l_act, 1)
            act.wait_ge(l_act, 1)
            act.activation(decay[:, 2:3], decay[:, 1:2], ACT.Exp, scale=-1.0).then_inc(l_act, 1)
            act.wait_ge(l_act, 2)
            act.activation(decay[:, 3:4], decay[:, 2:3], ACT.Ln, bias=1.0).then_inc(s_decay, 1)
            act.mul(bias_i[:], bias_i[:], 0.5)
            act.mul(bias_r[:], bias_r[:], 0.5).then_inc(s_bias, 1)
            act.wait_ge(s_bias, 1)
            act.wait_ge(s_decay, 2)
            act.wait_ge(s_const, 2)

            def mixer(g):
                act.wait_ge(pe_xnT, g + 1)
                ge(act, v_gated, g)
                ge(act, pe_z, g)
                act.copy(xnT[:], ps_xnT[:]).then_inc(a_xnT, 1)
                act.wait_ge(pe_z, g + 1)
                act.activation(ti[:], ps_zi[:], ACT.Tanh, bias=bias_i[:], scale=0.5)
                act.activation(tr[:], ps_zr[:], ACT.Tanh, bias=bias_r[:], scale=0.5).then_inc(l_act, 1)
                act.wait_ge(l_act, g * 2 + 3)
                ge(act, v_scan, g)
                act.activation(at[:], tr[:], ACT.Exp, bias=decay[:, 5:6], scale=decay[:, 5:6]).then_inc(a_at, 1)
                act.wait_ge(a_at, g + 1)
                act.activation(at2[:], at[:], ACT.Square).then_inc(l_act, 1)

            def std_first(g):
                act.wait_ge(v_var1, g + 1)
                act.activation(std1[:], mv1[:, :, 1], ACT.Sqrt, bias=eps_c[:]).then_inc(a_std1, 1)

            def root(g):
                act.wait_ge(l_act, g * 2 + 4)
                act.activation(bq[:], at2[:], ACT.Sqrt, bias=decay[:, 4:5], scale=-0.25).then_inc(a_gate, 1)

            def std_mixed(g):
                act.wait_ge(v_varh, g + 1)
                act.activation(stdh[:], mvh[:, :, 1], ACT.Sqrt, bias=eps_c[:]).then_inc(a_stdh, 1)

            def std_second(g):
                act.wait_ge(v_var2, g + 1)
                act.activation(std2[:], mv2[:, :, 1], ACT.Sqrt, bias=eps_c[:]).then_inc(a_std2, 1)

            def router(g):
                act.wait_ge(pe_x2T, g + 1)
                ge(act, pe_logit, g)
                act.copy(xn2T[:], ps_x2T[:]).then_inc(a_x2T, 1)
                act.copy(xn2_all[:, bass.ds(g * GT, GT), :], xn2[:]).then_inc(a_x2c, 1)
                act.wait_ge(pe_logit, g + 1)
                act.activation(th[:].rearrange("p j e -> p (j e)"), ps_logit[:, 0:GT * E], ACT.Tanh,
                               scale=0.5).then_inc(a_th, 1)

            def step(s, mix, nxt, old, route):
                if mix:
                    mixer(s)
                if nxt:
                    std_first(s + 1)
                if mix:
                    root(s)
                if old:
                    std_mixed(s - 1)
                if route:
                    std_second(s - 2)
                    router(s - 2)

            std_first(0)
            step(0, True, True, False, False)
            step(1, True, True, True, False)
            step(2, True, True, True, True)
            with act.Fori(3, G - 1) as s:
                step(s, True, True, True, True)
            step(G - 1, True, False, True, True)
            step(G, False, False, True, True)
            step(G + 1, False, False, False, True)

            for h in range(HALVES):
                steps = steps_value(act, h)
                act.preload_act_table(ACT.Tanh)
                with act.Fori(0, steps) as q:
                    for p in range(2):
                        act.wait_ge(b_gu[h], q * 2 + p + 1)
                        act.activation(act_t[:, p, :, :], ps_gu[p][:, 0:4 * I].rearrange(
                            "t (b w i) -> t b w i", b=2, w=2)[:, :, 0, :], ACT.Tanh, scale=0.5).then_inc(b_tanh[h], 1)
                    for p in range(2):
                        act.wait_ge(b_aT[h], q * 2 + p + 1)
                        act.copy(aT[:, p, :, :].rearrange("i b t -> i (b t)"), ps_aT[p][0:I, 0:2 * P]).then_inc(b_aTc[h], 1)

        @block.vector
        def _(dve):
            dve.wait_ge(s_small, 64)
            dve.memset(decay[:, 4:5], 0.25)
            dve.wait_ge(s_decay, 1)
            dve.scalar_tensor_tensor(out=decay[:, 5:6], in0=decay[:, 0:1], scalar=0.0, in1=decay[:, 3:4],
                                     op0=ALU.max, op1=ALU.add).then_inc(l_tab, 1)
            dve.wait_ge(l_tab, 1)
            dve.tensor_scalar(decay[:, 5:6], decay[:, 5:6], -4.0, None, ALU.mult).then_inc(s_decay, 1)
            dve.wait_ge(s_setT, 1)
            dve.tensor_copy(wiT[:], ps_setup[:, 0:P])
            dve.tensor_copy(wrT[:], ps_setup[:, P:2 * P])
            dve.tensor_copy(gateT[:], ps_setup[:, 2 * P:2 * P + E]).then_inc(s_wT, 1)
            dve.wait_ge(s_const, 2)

            def stats(source, st, mv, link, n):
                for j in range(GT):
                    ins = dve.bn_stats(st[:, j, :], source(j))
                ins.then_inc(link, 1)
                wait_apart(dve, link, n)
                for j in range(GT):
                    ins = dve.bn_aggr(mv[:, j, :], st[:, j, :])
                return ins

            def stats_first(g):
                wait_apart(dve, s_x, 16 * (g + 1))
                stats(lambda j: x_sb[:, bass.ds(g * GT + j, 1), :].rearrange("p a c -> p (a c)"),
                      st1, mv1, l_ln1, g * 2 + 1).then_inc(v_var1, 1)

            def norm_first(g):
                dve.wait_ge(a_std1, g + 1)
                dve.reciprocal(rstd1[:], std1[:]).then_inc(l_ln1, 1)
                dve.wait_ge(l_ln1, g * 2 + 2)
                ge(dve, pe_xnT, g)
                for j in range(GT):
                    ins = dve.tensor_scalar(xn[:, j, :], x_sb[:, bass.ds(g * GT + j, 1), :].rearrange("p a c -> p (a c)"),
                                            mv1[:, j, 0:1], rstd1[:, j:j + 1], ALU.subtract, ALU.mult)
                ins.then_inc(v_xn, 1)

            def recur(g):
                dve.wait_ge(a_gate, g + 1)
                dve.scalar_tensor_tensor(out=gated[:], in0=ti[:], scalar=1.0, in1=xnT[:],
                                         op0=ALU.add, op1=ALU.mult).then_inc(v_gated, 1)
                dve.wait_ge(v_gated, g + 1)
                dve.tensor_tensor(gx[:], bq[:], gated[:], ALU.mult).then_inc(l_scan, 1)
                dve.wait_ge(l_scan, g + 1)
                ge(dve, pe_h, g)
                for t in range(0, GC, SEQ):
                    ins = dve.tensor_tensor_scan(hT[:, t:t + SEQ], at[:, t:t + SEQ], gx[:, t:t + SEQ], 0.0,
                                                 ALU.mult, ALU.add)
                ins.then_inc(v_scan, 1)

            def stats_mixed(g):
                wait_apart(dve, pe_h, g + 1)
                stats(lambda j: ps_h[:, j * P:(j + 1) * P], sth, mvh, l_x1, g * 4 + 1).then_inc(v_varh, 1)

            def add_mixed(g):
                dve.wait_ge(a_stdh, g + 1)
                dve.reciprocal(rstdh[:], stdh[:]).then_inc(l_x1, 1)
                dve.wait_ge(l_x1, g * 4 + 2)
                for j in range(GT):
                    ins = dve.tensor_scalar(hn[:, j, :], ps_h[:, j * P:(j + 1) * P],
                                            mvh[:, j, 0:1], rstdh[:, j:j + 1], ALU.subtract, ALU.mult)
                ins.then_inc(l_x1, 1)
                dve.wait_ge(l_x1, g * 4 + 3)
                dve.tensor_tensor(x_sb[:, bass.ds(g * GT, GT), :], x_sb[:, bass.ds(g * GT, GT), :], hn[:],
                                  ALU.add).then_inc(v_x1, 1)
                wait_apart(dve, v_x1, g + 1)
                stats(lambda j: x_sb[:, bass.ds(g * GT + j, 1), :].rearrange("p a c -> p (a c)"),
                      st2, mv2, l_x1, g * 4 + 4).then_inc(v_var2, 1)

            def norm_second(g):
                dve.wait_ge(a_std2, g + 1)
                dve.reciprocal(rstd2[:], std2[:]).then_inc(l_route, 1)
                dve.wait_ge(l_route, g * DVE_ROUTE + 1)
                ge(dve, pe_x2T, g)
                ge(dve, a_x2c, g)
                for j in range(GT):
                    ins = dve.tensor_scalar(xn2[:, j, :], x_sb[:, bass.ds(g * GT + j, 1), :].rearrange("p a c -> p (a c)"),
                                            mv2[:, j, 0:1], rstd2[:, j:j + 1], ALU.subtract, ALU.mult)
                ins.then_inc(v_xn2, 1)

            def route(g):
                n = [1]

                def link(ins):
                    n[0] += 1
                    ins.then_inc(l_route, 1)
                    wait_apart(dve, l_route, g * DVE_ROUTE + n[0])

                dve.wait_ge(a_th, g + 1)
                link(dve.tensor_scalar(score[:], th[:], 0.5, 0.5, ALU.mult, ALU.add))
                link(dve.tensor_tensor(biased[:], score[:], ebias[:].unsqueeze(1).to_broadcast([P, GT, E]), ALU.add))
                for j in range(GT):
                    ins = dve.max(top[:, j, :], biased[:, j, :])
                link(ins)
                for j in range(GT):
                    ins = dve.max_index(top_i[:, j, :], top[:, j, :], biased[:, j, :])
                link(ins)
                link(dve.tensor_copy(top_f[:], top_i[:, :, 0:K]))
                hot = hot_all[:, bass.ds(g * GT, GT), :, :]
                link(dve.tensor_tensor(hot, iota_e[:].unsqueeze(1).unsqueeze(1).to_broadcast([P, GT, K, E]),
                                       top_f[:].unsqueeze(3).to_broadcast([P, GT, K, E]), ALU.is_equal))
                with nc.allow_low_precision(reason="a mask of zeros and ones"):
                    dve.tensor_reduce(mask[:], hot.rearrange("p j k e -> p j e k"), AX_X, ALU.add).then_inc(v_mask, 1)
                link(dve.tensor_tensor(picked[:], hot, score[:].unsqueeze(2).to_broadcast([P, GT, K, E]), ALU.mult))
                link(dve.tensor_reduce(wsel[:], picked[:], AX_X, ALU.add))
                link(dve.tensor_reduce(wsum[:], wsel[:], AX_X, ALU.add))
                link(dve.reciprocal(winv[:], wsum[:]))
                dve.scalar_tensor_tensor(out=wt_all[:, bass.ds(g * GT, GT), :], in0=wsel[:], scalar=0.5,
                                         in1=winv[:].unsqueeze(2).to_broadcast([P, GT, K]),
                                         op0=ALU.mult, op1=ALU.mult).then_inc(v_wt, 1)
                dve.wait_ge(pe_pos, g + 1)
                link(dve.tensor_tensor(pos[:], ps_pos[:, 0:GT * E].rearrange("p (j e) -> p j e", j=GT),
                                       region_e[:].unsqueeze(1).to_broadcast([P, GT, E]), ALU.add))
                link(dve.tensor_tensor(picked[:], hot, pos[:].unsqueeze(2).to_broadcast([P, GT, K, E]), ALU.mult))
                rows = row_f[:, bass.ds(g * GT, GT), :]
                link(dve.tensor_reduce(rows, picked[:], AX_X, ALU.add))
                dve.tensor_copy(row_xs[:, bass.ds(g * GT * K, GT * K)].rearrange("p (j k) -> p j k", j=GT),
                                rows).then_inc(v_row, 1)
                link(dve.tensor_reduce(add4[:], mask[:].rearrange("p j e -> p e j"), AX_X, ALU.add))
                with nc.allow_low_precision(reason="counts of at most 16"):
                    dve.tensor_tensor(seen[:], seen[:], add4[:], ALU.add).then_inc(v_seen, 1)
                assert n[0] == DVE_ROUTE

            def tables(h):
                n = [h * DVE_TABLES + 1]

                def link(ins):
                    n[0] += 1
                    ins.then_inc(l_tab, 1)
                    dve.wait_ge(l_tab, n[0])

                dve.wait_ge(pe_cnt, h + 1)
                link(dve.tensor_copy(cnt[:], ps_pos[:, 128:128 + E]))
                if h + 1 < HALVES:
                    dve.wait_ge(v_seen, (h + 1) * GH)
                    dve.memset(seen[:], 0.0).then_inc(v_seen, 1)
                link(dve.tensor_scalar(cnt_up[:], cnt[:], float(P - 1), None, ALU.add))
                link(dve.tensor_scalar(nblk_i[:], cnt_up[:], 7, None, ALU.logical_shift_right))
                link(dve.tensor_copy(nblk[:], nblk_i[:]))
                link(dve.tensor_tensor_scan(cum[:], ones_e[:], nblk[:], 0.0, ALU.mult, ALU.add))
                link(dve.tensor_scalar(past[:], cum[:], iota_p[:], None, ALU.is_le))
                link(dve.tensor_tensor(past_n[:], past[:], nblk[:], ALU.mult))
                link(dve.tensor_reduce(tcol[:, 0:1], past[:], AX_X, ALU.add))
                link(dve.tensor_reduce(tcol[:, 1:2], past_n[:], AX_X, ALU.add))
                link(dve.tensor_scalar(tcol[:, 2:3], tcol[:, 0:1], float(E - 1), None, ALU.min))
                link(dve.tensor_tensor(tcol[:, 3:4], iota_p[:], tcol[:, 1:2], ALU.subtract))
                link(dve.tensor_scalar(tcol[:, 4:5], tcol[:, 3:4], float(P), None, ALU.mult))
                link(dve.scalar_tensor_tensor(out=tcol[:, 5:6], in0=tcol[:, 0:1], scalar=float(REGION), in1=tcol[:, 4:5],
                                              op0=ALU.mult, op1=ALU.add))
                dve.tensor_tensor(past_n[:], cnt[:], region_e[:], ALU.add).then_inc(v_tcol, 1)
                link(dve.tensor_scalar(steps_u[:, 0:1], cum[0:1, E - 1:E], float(SLOTS - 1), None, ALU.add))
                link(dve.tensor_scalar(steps_of[h][:], steps_u[:, 0:1], SLOTS.bit_length() - 1, None, ALU.logical_shift_right))
                dve.wait_ge(v_tcol, h + 1)
                dve.tensor_copy(tail_of[h][:], past_n[0:1, :])
                dve.wait_ge(pe_tab, h + 1)
                link(dve.tensor_copy(expert_of[h][:], ps_setup[0:1, 0:P]))
                dve.tensor_copy(row_of[h][:], ps_setup[0:1, P:2 * P]).then_inc(v_tab, 1)
                link(dve.tensor_tensor(past[:], cum[:], nblk[:], ALU.subtract))
                link(dve.scalar_tensor_tensor(out=pack[:], in0=past[:], scalar=float(P), in1=region_e[:],
                                              op0=ALU.mult, op1=ALU.subtract))
                for g in range(h * GH, (h + 1) * GH):
                    link(dve.tensor_tensor(picked[:], hot_all[:, g * GT:(g + 1) * GT, :, :],
                                           pack[:].unsqueeze(1).unsqueeze(1).to_broadcast([P, GT, K, E]), ALU.mult))
                    link(dve.tensor_reduce(wsel[:], picked[:], AX_X, ALU.add))
                    dve.tensor_tensor(row_ys[:, g * GT * K:(g + 1) * GT * K].rearrange("p (j k) -> p j k", j=GT),
                                      row_f[:, g * GT:(g + 1) * GT, :], wsel[:], ALU.add).then_inc(v_pack, 1)
                assert n[0] == (h + 1) * DVE_TABLES + 1

            def step(s, mix, nxt, old, rt):
                if mix:
                    norm_first(s)
                if old:
                    stats_mixed(s - 1)
                if nxt:
                    stats_first(s + 1)
                if rt:
                    norm_second(s - 2)
                if old:
                    add_mixed(s - 1)
                if mix:
                    recur(s)
                if rt:
                    route(s - 2)

            stats_first(0)
            step(0, True, True, False, False)
            step(1, True, True, True, False)
            step(2, True, True, True, True)
            with dve.Fori(3, GH + 2) as s:
                step(s, True, True, True, True)
            tables(0)
            with dve.Fori(GH + 2, G - 1) as s:
                step(s, True, True, True, True)
            step(G - 1, True, False, True, True)
            step(G, False, False, True, True)
            step(G + 1, False, False, False, True)
            tables(1)

            for h in range(HALVES):
                steps = steps_value(dve, h)
                if h:
                    for u in range(SLOTS):
                        wait_apart(dve, s_ys[0][u], steps_before * 16 + 16)
                steps_before = steps
                with dve.Fori(0, steps) as q:
                    for p in range(2):
                        dve.wait_ge(b_xT[h], q * 4 + p * 2 + 2)
                        dve.tensor_copy(xbT[:, p, :, :].rearrange("c b t -> c (b t)"), ps_xbT[p][:, 0:2 * P]).then_inc(b_xTc[h], 1)
                    for p in range(2):
                        gu = ps_gu[p][:, 0:4 * I].rearrange("t (b w i) -> t b w i", b=2, w=2)
                        dve.wait_ge(b_tanh[h], q * 2 + p + 1)
                        dve.scalar_tensor_tensor(out=silu2[:, p, :, :], in0=act_t[:, p, :, :], scalar=1.0,
                                                 in1=gu[:, :, 0, :], op0=ALU.add, op1=ALU.mult).then_inc(b_silu[h], 1)
                        dve.wait_ge(b_silu[h], q * 2 + p + 1)
                        dve.tensor_tensor(act_a[:, p, :, :], silu2[:, p, :, :], gu[:, :, 1, :], ALU.mult).then_inc(b_act[h], 1)
                    for p in range(2):
                        dve.wait_ge(b_y[h], q * 2 + p + 1)
                        for u in range(2 * p, 2 * p + 2):
                            dve.wait_ge(s_ys[h][u], q * 16 + 16)
                        dve.tensor_copy(yb[:, 2 * p:2 * p + 2, :].rearrange("t b c -> t (b c)"),
                                        ps_y[p][:, 0:2 * P]).then_inc(b_yc[h], 1)

            def combine(g, h):
                b = g % 2
                n = [g * 6]

                def link(ins):
                    n[0] += 1
                    ins.then_inc(l_mix, 1)
                    dve.wait_ge(l_mix, n[0])

                if g >= 2:
                    dve.wait_ge(c_fin, g - 1)
                dve.wait_ge(s_yk[b], 16 * GT * K * (g // 2 + 1))
                for k in range(K):
                    for j in range(GT):
                        t = g * GT + j
                        y = yk[h][:, t - h * TH, k, :]
                        if k == 0:
                            ins = dve.tensor_scalar(mix[:, b, j, :], y, wt_all[:, t, 0:1], None, ALU.mult)
                        else:
                            ins = dve.scalar_tensor_tensor(out=mix[:, b, j, :], in0=y, scalar=wt_all[:, t, k:k + 1],
                                                           in1=mix[:, b, j, :], op0=ALU.mult, op1=ALU.add)
                    link(ins)
                stats(lambda j: mix[:, b, j, :], st3, mv3[:, b, :, :], l_mix, n[0] + 1).then_inc(l_mix, 1)
                n[0] += 2
                dve.wait_ge(l_mix, n[0])
                dve.tensor_scalar(ve3[:, b, :], mv3[:, b, :, 1], EPS, None, ALU.add).then_inc(c_ve, 1)

            def finish(g):
                b = g % 2
                dve.wait_ge(c_pow, g + 1)
                if g >= 2:
                    dve.wait_ge(s_out[b], 16 * (g // 2))
                for j in range(GT):
                    dve.tensor_scalar(mix[:, b, j, :], mix[:, b, j, :], mv3[:, b, j, 0:1], rstd3[:, b, j:j + 1],
                                      ALU.subtract, ALU.mult).then_inc(s_fin, 1)
                dve.wait_ge(s_fin, GT * (g + 1))
                dve.tensor_tensor(fin[:, b, :, :], mix[:, b, :, :], x_sb[:, g * GT:(g + 1) * GT, :],
                                  ALU.add).then_inc(c_fin, 1)

            for g in range(G):
                combine(g, g // GH)
                if g:
                    finish(g - 1)
            finish(G - 1)

        @block.tensor
        def _(pe):
            pe.wait_ge(s_const, 2)
            pe.wait_ge(s_wmix, 48)
            pe.transpose(ps_setup[:, 0:P], wi_raw[:], ident[:])
            pe.transpose(ps_setup[:, P:2 * P], wr_raw[:], ident[:])
            pe.transpose(ps_setup[:, 2 * P:2 * P + E], gate_raw[:], ident[0:E, 0:E]).then_inc(s_setT, 1)
            pe.wait_ge(s_wT, 1)

            def mixer(g):
                pe.wait_ge(v_xn, g + 1)
                ge(pe, a_xnT, g)
                for j in range(GT):
                    ins = pe.transpose(ps_xnT[:, j * P:(j + 1) * P], xn[:, j, :], ident[:])
                ins.then_inc(pe_xnT, 1)
                pe.wait_ge(a_xnT, g + 1)
                pe.matmul(ps_zi[:], wiT[:], xnT[:], start=True, stop=True)
                pe.matmul(ps_zr[:], wrT[:], xnT[:], start=True, stop=True).then_inc(pe_z, 1)

            def mixed(g):
                pe.wait_ge(v_scan, g + 1)
                for j in range(GT):
                    ins = pe.transpose(ps_h[:, j * P:(j + 1) * P], hT[:, j * P:(j + 1) * P], ident[:])
                ins.then_inc(pe_h, 1)

            def router(g):
                pe.wait_ge(v_xn2, g + 1)
                ge(pe, a_x2T, g)
                for j in range(GT):
                    ins = pe.transpose(ps_x2T[:, j * P:(j + 1) * P], xn2[:, j, :], ident[:])
                ins.then_inc(pe_x2T, 1)
                pe.wait_ge(a_x2T, g + 1)
                for j in range(GT):
                    ins = pe.matmul(ps_logit[:, j * E:(j + 1) * E], xn2T[:, j * P:(j + 1) * P], gateT[:],
                                    start=True, stop=True)
                ins.then_inc(pe_logit, 1)

            def positions(g, reset):
                pe.wait_ge(v_mask, g + 1)
                ge(pe, v_seen, g + reset)
                for j in range(GT):
                    dst = ps_pos[:, j * E:(j + 1) * E]
                    pe.matmul(dst, ones[:], seen[:], start=True, stop=False)
                    for i in range(j):
                        pe.matmul(dst, ones[:], mask[:, i, :], start=False, stop=False)
                    ins = pe.matmul(dst, before[:], mask[:, j, :], start=False, stop=True)
                ins.then_inc(pe_pos, 1)

            def tables(h):
                pe.wait_ge(v_seen, (h + 1) * GH + h)
                pe.matmul(ps_pos[:, 128:128 + E], ones[:], seen[:], start=True, stop=True).then_inc(pe_cnt, 1)
                pe.wait_ge(v_tcol, h + 1)
                pe.transpose(ps_setup[0:1, 0:P], tcol[:, 2:3], ident[:])
                pe.transpose(ps_setup[0:1, P:2 * P], tcol[:, 5:6], ident[:]).then_inc(pe_tab, 1)

            def step(s, mix, rt, reset=0):
                if mix:
                    mixer(s)
                if rt:
                    router(s - 2)
                if mix:
                    mixed(s)
                if rt:
                    positions(s - 2, reset)

            step(0, True, False)
            step(1, True, False)
            step(2, True, True)
            with pe.Fori(3, GH + 2) as s:
                step(s, True, True)
            tables(0)
            with pe.Fori(GH + 2, G) as s:
                step(s, True, True, 1)
            step(G, False, True, 1)
            step(G + 1, False, True, 1)
            tables(1)

            pe.wait_ge(s_wexp, 48)
            for h in range(HALVES):
                steps = steps_value(pe, h)
                with pe.Fori(0, steps) as q:
                    e_of = [pe.value_load(expert_of[h][0:1, bass.ds(q * SLOTS + u, 1)], min_val=0, max_val=E - 1)
                            for u in range(SLOTS)]
                    for u in range(SLOTS):
                        pe.wait_ge(s_xb[h][u], q * 16 + 16)
                        pe.transpose(ps_xbT[u // 2][:, (u % 2) * P:(u % 2 + 1) * P], xb[:, u, :], ident[:]).then_inc(b_xT[h], 1)
                    for u in range(SLOTS):
                        if u % 2 == 0:
                            pe.wait_ge(b_xTc[h], q * 2 + u // 2 + 1)
                        ins = pe.matmul(ps_gu[u // 2][:, (u % 2) * 2 * I:(u % 2 + 1) * 2 * I], xbT[:, u // 2, u % 2, :],
                                        w13_sb[:, bass.ds(e_of[u], 1), :, :].rearrange("c a w i -> c (a w i)"),
                                        start=True, stop=True)
                        if u % 2:
                            ins.then_inc(b_gu[h], 1)
                    for u in range(SLOTS):
                        if u % 2 == 0:
                            pe.wait_ge(b_act[h], q * 2 + u // 2 + 1)
                        ins = pe.transpose(ps_aT[u // 2][0:I, (u % 2) * P:(u % 2 + 1) * P], act_a[:, u // 2, u % 2, :], ident[:])
                        if u % 2:
                            ins.then_inc(b_aT[h], 1)
                    for u in range(SLOTS):
                        if u % 2 == 0:
                            pe.wait_ge(b_aTc[h], q * 2 + u // 2 + 1)
                        ins = pe.matmul(ps_y[u // 2][:, (u % 2) * P:(u % 2 + 1) * P], aT[:, u // 2, u % 2, :],
                                        w2_sb[:, bass.ds(e_of[u], 1), :].rearrange("i a c -> i (a c)"),
                                        start=True, stop=True)
                        if u % 2:
                            ins.then_inc(b_y[h], 1)


_INS = ["L0_attn_x", "L0_attn_Wi", "L0_attn_bi", "L0_attn_Wr", "L0_attn_br", "L0_attn_cap_lambda",
        "L0_ffn_gate_w", "L0_ffn_w1", "L0_ffn_w3", "L0_ffn_w2", "L0_ffn_e_bias"]


def kernel(**inputs):
    import numpy as _np
    import concourse.bacc as _bacc
    from concourse import mybir as _mybir
    from concourse.bass_utils import run_bass_kernel_spmd as _run

    nc = _bacc.Bacc("TRN2", target_bir_lowering=False, num_devices=1)
    arrays, args = {}, []
    for name in _INS:
        a = _np.ascontiguousarray(inputs[name])
        arrays[f"in_{name}_dram"] = a
        args.append(nc.dram_tensor(f"in_{name}_dram", a.shape, _mybir.dt.from_np(a.dtype), kind="ExternalInput").ap())
    shape = inputs["L0_attn_x"].shape
    experts = inputs["L0_ffn_gate_w"].shape[0]
    fp32 = _mybir.dt.float32
    args.append(nc.dram_tensor("out_0_dram", shape, fp32, kind="ExternalOutput").ap())
    tokens = shape[0] * shape[1] // HALVES
    blocks = -(-(tokens * K // P + experts - 1) // SLOTS) * SLOTS
    for kind, rows in (("xs", (experts + 1) * (tokens + P)), ("ys", blocks * P)):
        args.append([nc.dram_tensor(f"{kind}{h}_dram", (rows, shape[2]), fp32, kind="Internal").ap() for h in range(HALVES)])
    sandwich_kernel(nc, *args)
    r = _run(nc, [arrays], core_ids=[0])
    return r.results[0]["out_0_dram"]
```

```python
from contextlib import ExitStack

import concourse.bass as bass
from concourse import mybir

ALU = mybir.AluOpType
ACT = mybir.ActivationFunctionType
AX_X = mybir.AxisListType.X
F32 = mybir.dt.float32
BF16 = mybir.dt.bfloat16
F16 = mybir.dt.float16
U32 = mybir.dt.uint32
I32 = mybir.dt.int32

P = 128
EPS = 1e-5
K = 4
GT = 4
HALVES = 2
SLOTS = 4
DVE_TABLES = 26
DVE_ROUTE = 15


def sandwich_kernel(nc: bass.Bass, x, Wi, bi, Wr, br, cap, gate_w, w1, w3, w2, e_bias, out, xs, ys):
    B, T, C = x.shape
    E, _, I = w1.shape
    TILES = B * T // P
    G = TILES // GT
    GH = G // HALVES
    TH = TILES // HALVES
    GC = GT * P
    SEQ = T
    REGION = TH * P + P
    MAX_BLOCKS = ys[0].shape[0] // P
    assert C == P and GC % SEQ == 0

    x_rows = x.rearrange("b t c -> (b t) c").rearrange("(n p) c -> p n c", p=P)
    out_rows = out.rearrange("b t c -> (b t) c").rearrange("(n p) c -> p n c", p=P)

    with ExitStack() as ctx:
        def sb(name, shape, dt=F32):
            return ctx.enter_context(nc.sbuf_tensor(name, shape, dt))

        def sem(name):
            return ctx.enter_context(nc.semaphore(name))

        bank = [ctx.enter_context(nc.psum_tensor(f"bank{i}", [P, 512], F32)) for i in range(8)]
        ps_xnT, ps_zi, ps_zr, ps_h, ps_x2T, ps_logit, ps_pos = bank[:7]
        ps_setup = bank[7]
        ps_xbT, ps_gu, ps_aT, ps_y = (bank[2 * i:2 * i + 2] for i in range(4))

        wi_raw, wr_raw, gate_raw = sb("wi_raw", [P, C]), sb("wr_raw", [P, C]), sb("gate_raw", [E, C])
        wiT, wrT, gateT = sb("wiT", [C, P]), sb("wrT", [C, P]), sb("gateT", [C, E])
        w13_h, w13_l = sb("w13_h", [C, E, 2, I], F16), sb("w13_l", [C, E, 2, I], F16)
        w2_h, w2_l = sb("w2_h", [I, E, C], F16), sb("w2_l", [I, E, C], F16)
        wmax, wtop = sb("wmax", [P, 2]), sb("wtop", [1, 2])
        wpow, wrow, wscale = sb("wpow", [1, 2]), sb("wrow", [1, 8]), sb("wscale", [P, 8])
        ones_row = sb("ones_row", [1, P])
        ident_h = sb("ident_h", [P, P], F16)
        bias_i, bias_r, decay = sb("bias_i", [P, 1]), sb("bias_r", [P, 1]), sb("decay", [P, 6])
        ebias = sb("ebias", [P, E])
        ident = sb("ident", [P, P])
        before = sb("before", [P, P], BF16)
        ones = sb("ones", [P, P], BF16)
        iota_e, region_e, iota_p = sb("iota_e", [P, E]), sb("region_e", [P, E]), sb("iota_p", [P, 1])
        eps_c, neg_half = sb("eps_c", [P, 1]), sb("neg_half", [P, GT])
        zeros = sb("zeros", [P, P])

        x_sb = sb("x_sb", [P, TILES, C])
        xn2_all = sb("xn2_all", [P, TILES, C])
        row_xs, row_ys = sb("row_xs", [P, TILES * K], U32), sb("row_ys", [P, TILES * K], U32)
        row_f = sb("row_f", [P, TILES, K])
        wt_all = sb("wt_all", [P, TILES, K])

        st1, mv1, std1 = sb("st1", [P, GT, 6]), sb("mv1", [P, GT, 2]), sb("std1", [P, GT])
        rstd1, xn, xnT = sb("rstd1", [P, GT]), sb("xn", [P, GT, C]), sb("xnT", [C, GC])
        ti, tr, at, at2, bq = (sb(n, [P, GC]) for n in ("ti", "tr", "at", "at2", "bq"))
        gated, gx, hT = sb("gated", [P, GC]), sb("gx", [P, GC]), sb("hT", [P, GC])
        sth, mvh, stdh = sb("sth", [P, GT, 6]), sb("mvh", [P, GT, 2]), sb("stdh", [P, GT])
        rstdh, hn = sb("rstdh", [P, GT]), sb("hn", [P, GT, C])
        st2, mv2, std2 = sb("st2", [P, GT, 6]), sb("mv2", [P, GT, 2]), sb("std2", [P, GT])
        rstd2, xn2, xn2T = sb("rstd2", [P, GT]), sb("xn2", [P, GT, C]), sb("xn2T", [C, GC])
        th, score, biased = sb("th", [P, GT, E]), sb("score", [P, GT, E]), sb("biased", [P, GT, E])
        top, top_i, top_f = sb("top", [P, GT, 8]), sb("top_i", [P, GT, 8], U32), sb("top_f", [P, GT, K])
        hot_all, picked = sb("hot_all", [P, TILES, K, E], BF16), sb("picked", [P, GT, K, E])
        mask, seen, add4 = sb("mask", [P, GT, E], BF16), sb("seen", [P, E], BF16), sb("add4", [P, E])
        pos = sb("pos", [P, GT, E])
        wsel, wsum, winv = sb("wsel", [P, GT, K]), sb("wsum", [P, GT]), sb("winv", [P, GT])

        cnt, cnt_up, nblk_i, nblk = sb("cnt", [P, E]), sb("cnt_up", [P, E], I32), sb("nblk_i", [P, E], I32), sb("nblk", [P, E])
        pack = sb("pack", [P, E])
        cum, past, past_n = sb("cum", [P, E]), sb("past", [P, E]), sb("past_n", [P, E])
        ones_e = sb("ones_e", [P, E])
        tcol = sb("tcol", [P, 8])
        steps_f, steps_u = sb("steps_f", [1, 2]), sb("steps_u", [1, 2], I32)
        expert_of = [sb(f"expert_of{h}", [1, P], I32) for h in range(HALVES)]
        row_of = [sb(f"row_of{h}", [1, P], I32) for h in range(HALVES)]
        tail_of = [sb(f"tail_of{h}", [1, E], I32) for h in range(HALVES)]
        steps_of = [sb(f"steps_of{h}", [1, 1], I32) for h in range(HALVES)]

        xb = sb("xb", [P, SLOTS, C])
        xbT_h, xbT_l = sb("xbT_h", [C, 2, 2, P], F16), sb("xbT_l", [C, 2, 2, P], F16)
        act_t, silu2, act_a = (sb(n, [P, 2, 2, I]) for n in ("act_t", "silu2", "act_a"))
        act_h, act_l = sb("act_h", [P, 2, 2, I], F16), sb("act_l", [P, 2, 2, I], F16)
        aT, yb = sb("aT", [I, 2, 2, 2, P], F16), sb("yb", [P, 2, 2, C])

        yk = [sb(f"yk{h}", [P, TH, K, C]) for h in range(HALVES)]
        w13_raw = yk[1][:].rearrange("p t k c -> p (t k c)")[:, 0:E * 2 * I].rearrange("p (e w i) -> p e w i", e=E, w=2)
        w2_raw = yk[0][:].rearrange("p t k c -> p (t k c)")[0:I, 0:E * C].rearrange("p (e c) -> p e c", e=E)
        mix = sb("mix", [P, 2, GT, C])
        st3, mv3, ve3, rstd3 = sb("st3", [P, GT, 6]), sb("mv3", [P, 2, GT, 2]), sb("ve3", [P, 2, GT]), sb("rstd3", [P, 2, GT])

        s_wmix, s_wexp, s_small, s_x = sem("s_wmix"), sem("s_wexp"), sem("s_small"), sem("s_x")
        s_const, s_z0, s_setT, s_wT, s_bias, s_decay = (sem(n) for n in (
            "s_const", "s_z0", "s_setT", "s_wT", "s_bias", "s_decay"))
        v_var1, a_std1, v_xn, pe_xnT, a_xnT, pe_z, a_at, a_gate, v_gated, v_scan, pe_h = (sem(n) for n in (
            "v_var1", "a_std1", "v_xn", "pe_xnT", "a_xnT", "pe_z", "a_at", "a_gate", "v_gated", "v_scan", "pe_h"))
        v_varh, a_stdh, v_x1, v_var2, a_std2 = (sem(n) for n in ("v_varh", "a_stdh", "v_x1", "v_var2", "a_std2"))
        v_xn2, pe_x2T, a_x2T, a_x2c, pe_logit, a_th, v_mask, pe_pos, v_row, v_wt, v_seen = (sem(n) for n in (
            "v_xn2", "pe_x2T", "a_x2T", "a_x2c", "pe_logit", "a_th", "v_mask", "pe_pos", "v_row", "v_wt", "v_seen"))
        l_ln1, l_scan, l_x1, l_route, l_act, l_tab, l_mix = (sem(n) for n in (
            "l_ln1", "l_scan", "l_x1", "l_route", "l_act", "l_tab", "l_mix"))
        s_scat = [sem(f"s_scat{h}") for h in range(HALVES)]
        v_pack = sem("v_pack")
        pe_cnt, v_tcol, pe_tab, v_tab = sem("pe_cnt"), sem("v_tcol"), sem("pe_tab"), sem("v_tab")
        s_fill = [sem(f"s_fill{h}") for h in range(HALVES)]
        s_tail = [sem(f"s_tail{h}") for h in range(HALVES)]
        s_xb = [[sem(f"s_xb{h}_{u}") for u in range(SLOTS)] for h in range(HALVES)]
        s_ys = [[sem(f"s_ys{h}_{p}") for p in range(2)] for h in range(HALVES)]
        b_xT, b_xh, b_xl, b_gu, b_tanh, b_silu, b_act, b_ah, b_al, b_aT, b_aTc, b_y, b_yc = (
            [sem(f"{n}{h}") for h in range(HALVES)] for n in (
                "b_xT", "b_xh", "b_xl", "b_gu", "b_tanh", "b_silu", "b_act", "b_ah", "b_al", "b_aT", "b_aTc", "b_y", "b_yc"))
        v_wmax, pe_wmax, v_wrow, pe_wrow, v_wscale, a_wh, v_wl = (sem(n) for n in (
            "v_wmax", "pe_wmax", "v_wrow", "pe_wrow", "v_wscale", "a_wh", "v_wl"))
        s_yk = [sem("s_yk0"), sem("s_yk1")]
        c_ve, c_pow, s_fin, c_fin = sem("c_ve"), sem("c_pow"), sem("s_fin"), sem("c_fin")
        s_out = sem("s_out")

        def ge(eng, s, n):
            if not isinstance(n, int) or n > 0:
                eng.wait_ge(s, n)

        def wait_apart(eng, s, n):
            if not isinstance(n, int):
                eng.to_reg(n)
            eng.wait_ge(s_const, 2)
            eng.wait_ge(s, n)

        def steps_value(eng, h):
            eng.wait_ge(v_tab, h + 1)
            return eng.value_load(steps_of[h][0:1, 0:1], min_val=TH * K // SLOTS - 3, max_val=MAX_BLOCKS // SLOTS - 3)

        def rows_loader(eng, name, n):
            regs = [eng.alloc_register(f"{name}{i}") for i in range(n)]

            def load(table, at, top):
                eng.load(regs, table[0:1, bass.ds(at, n)])
                return [eng.snap(r, min_val=0, max_val=top) for r in regs]
            return load

        def stages(t=6, left=-1):
            return [n <= t and n > left for n in range(7)]

        block = ctx.enter_context(nc.Block())

        @block.sync
        def _(sp):
            sp.dma_start(x_sb[:, 0:GT, :], x_rows[:, 0:GT, :]).then_inc(s_x, 16)
            sp.dma_start(wi_raw[:], Wi).then_inc(s_wmix, 16)
            sp.dma_start(wr_raw[:], Wr).then_inc(s_wmix, 16)
            sp.dma_start(gate_raw[:], gate_w).then_inc(s_wmix, 16)
            with nc.allow_non_contiguous_dma(reason="one bias per channel"):
                sp.dma_start(bias_i[:], bi.rearrange("(p a) -> p a", a=1)).then_inc(s_small, 16)
                sp.dma_start(bias_r[:], br.rearrange("(p a) -> p a", a=1)).then_inc(s_small, 16)
                sp.dma_start(decay[:, 0:1], cap.rearrange("(a b) -> a b", a=1).to_broadcast([P, 1])).then_inc(s_small, 16)
                sp.dma_start(ebias[:], e_bias.rearrange("(a b) -> a b", a=1).to_broadcast([P, E])).then_inc(s_small, 16)
            for g in range(1, G):
                sp.wait_ge(s_x, 16 * g)
                sp.dma_start(x_sb[:, g * GT:(g + 1) * GT, :], x_rows[:, g * GT:(g + 1) * GT, :]).then_inc(s_x, 16)
            sp.wait_ge(s_const, 2)
            for h in range(HALVES):
                sp.dma_start(xs[h][E * REGION:E * REGION + SLOTS * P, :].rearrange("(n p) c -> p n c", p=P),
                             zeros[:].unsqueeze(1).to_broadcast([P, SLOTS, C])).then_inc(s_fill[h], 16)
                sp.dma_start(ys[h].rearrange("(n p) c -> p n c", p=P)[:, TH * K:, :],
                             zeros[:].unsqueeze(1).to_broadcast([P, MAX_BLOCKS - TH * K, C])).then_inc(s_fill[h], 16)
            four = rows_loader(sp, "row", SLOTS)

            def zero_tails(h):
                sp.wait_ge(v_tab, h + 1)
                with sp.Fori(0, E // 4) as e:
                    for r in four(tail_of[h], e * 4, E * REGION - P):
                        sp.dma_start(xs[h][bass.ds(r, P), :], zeros[:]).then_inc(s_tail[h], 16)

            def blocks(h, most_before):
                sp.wait_ge(s_fill[h], 32)
                sp.wait_ge(s_tail[h], 16 * E)
                sp.wait_ge(s_scat[h], 16 * TH * K)
                most = steps_value(sp, h)
                top = (E + 1) * REGION - P

                def load(r, u):
                    sp.dma_start(xb[:, u, :], xs[h][bass.ds(r, P), :]).then_inc(s_xb[h][u], 16)

                def store(q, p):
                    sp.wait_ge(b_yc[h], q * 2 + p + 1)
                    sp.dma_start(ys[h][bass.ds((q * SLOTS + 2 * p) * P, 2 * P), :].rearrange("(b p) c -> p b c", p=P),
                                 yb[:, p, :, :]).then_inc(s_ys[h][p], 16)

                def step(q, stored):
                    rows = four(row_of[h], q * SLOTS + SLOTS, top)
                    for p in range(2):
                        sp.wait_ge(b_xT[h], q * 2 + p + 1)
                        for u in (2 * p, 2 * p + 1):
                            load(rows[u], u)
                        if stored is not None:
                            store(stored, p)

                rows = four(row_of[h], 0, top)
                if h:
                    wait_apart(sp, b_xT[h - 1], most_before * 2 + 6)
                for u in range(SLOTS):
                    load(rows[u], u)
                step(0, None)
                step(1, None)
                with sp.Fori(0, most) as q:
                    step(q + 2, q)
                for q in range(3):
                    for p in range(2):
                        store(most + q, p)
                return most

            zero_tails(0)
            zero_tails(1)
            most_before = None
            for h in range(HALVES):
                most_before = blocks(h, most_before)
            for h in range(HALVES):
                for g in range(h * GH, h * GH + GH):
                    sp.wait_ge(c_fin, g + 1)
                    sp.dma_start(out_rows[:, g * GT:(g + 1) * GT, :], x_sb[:, g * GT:(g + 1) * GT, :]).then_inc(s_out, 16)
            sp.wait_ge(s_out, 16 * G)

        @block.gpsimd
        def _(pool):
            pool.memset(zeros[:], 0.0).then_inc(s_const, 1)
            pool.memset(ident[:], 0.0).then_inc(s_z0, 1)
            pool.memset(before[:], 1.0).then_inc(s_z0, 1)
            pool.memset(ones[:], 1.0)
            pool.memset(eps_c[:], EPS)
            pool.memset(neg_half[:], -0.5)
            pool.memset(ones_e[:], 1.0)
            pool.memset(seen[:], 0.0)
            pool.memset(ones_row[:], 1.0)
            pool.memset(wmax[:], 0.0)
            pool.iota(iota_e[:], pattern=[[1, E]], base=0, channel_multiplier=0, allow_small_or_imprecise_dtypes=True)
            pool.iota(region_e[:], pattern=[[REGION, E]], base=0, channel_multiplier=0, allow_small_or_imprecise_dtypes=True)
            pool.iota(iota_p[:], pattern=[[0, 1]], base=0, channel_multiplier=1, allow_small_or_imprecise_dtypes=True)
            pool.wait_ge(s_z0, 2)
            pool.affine_select(out=ident[:], in_=ident[:], compare_op=ALU.not_equal, fill=1.0, base=0,
                               pattern=[[-1, P]], channel_multiplier=1)
            pool.affine_select(out=before[:], in_=before[:], compare_op=ALU.is_ge, fill=0.0, base=-1,
                               pattern=[[1, P]], channel_multiplier=-1).then_inc(s_const, 1)
            for h in range(HALVES):
                for g in range(h * GH, h * GH + GH):
                    pool.wait_ge(v_row, g + 1)
                    pool.wait_ge(a_x2c, g + 1)
                    for j in range(GT):
                        for k in range(K):
                            pool.indirect_dma_start(
                                out=xs[h], out_offset=bass.IndirectOffsetOnAxis(
                                    ap=row_xs[:, (g * GT + j) * K + k:(g * GT + j) * K + k + 1], axis=0),
                                in_=xn2_all[:, g * GT + j, :],
                                in_offset=None).then_inc(s_scat[h], 16)
            for h in range(HALVES):
                steps = steps_value(pool, h)
                for p in range(2):
                    wait_apart(pool, s_ys[h][p], steps * 16 + 48)
                pool.wait_ge(v_wl, 1)
                pool.wait_ge(v_pack, (h + 1) * GH)
                for g in range(h * GH, h * GH + GH):
                    for j in range(GT):
                        for k in range(K):
                            pool.indirect_dma_start(
                                out=yk[h][:, g * GT + j - h * TH, k, :], out_offset=None, in_=ys[h],
                                in_offset=bass.IndirectOffsetOnAxis(ap=row_ys[:, (g * GT + j) * K + k:(g * GT + j) * K + k + 1], axis=0),
                            ).then_inc(s_yk[g % 2], 16)
                    if g == G - 1:
                        for p in (g - 1, g):
                            pool.wait_ge(c_ve, p + 1)
                            pool.tensor_tensor(out=rstd3[:, p % 2, :], in0=ve3[:, p % 2, :], in1=neg_half[:],
                                               op=ALU.pow).then_inc(c_pow, 1)
                    elif g:
                        pool.wait_ge(c_ve, g)
                        pool.tensor_tensor(out=rstd3[:, (g - 1) % 2, :], in0=ve3[:, (g - 1) % 2, :], in1=neg_half[:],
                                           op=ALU.pow).then_inc(c_pow, 1)

        @block.scalar
        def _(act):
            act.dma_start(w13_raw[:, :, 0, :], w1.rearrange("e h i -> h e i")).then_inc(s_wexp, 16)
            act.dma_start(w13_raw[:, :, 1, :], w3.rearrange("e h i -> h e i")).then_inc(s_wexp, 16)
            act.dma_start(w2_raw, w2.rearrange("e i h -> i e h")).then_inc(s_wexp, 16)
            act.wait_ge(s_small, 64)
            act.activation(decay[:, 1:2], decay[:, 0:1], ACT.Abs).then_inc(l_act, 1)
            act.wait_ge(l_act, 1)
            act.activation(decay[:, 2:3], decay[:, 1:2], ACT.Exp, scale=-1.0).then_inc(l_act, 1)
            act.wait_ge(l_act, 2)
            act.activation(decay[:, 3:4], decay[:, 2:3], ACT.Ln, bias=1.0).then_inc(s_decay, 1)
            act.mul(bias_i[:], bias_i[:], 0.5)
            act.mul(bias_r[:], bias_r[:], 0.5).then_inc(s_bias, 1)
            act.wait_ge(s_bias, 1)
            act.wait_ge(s_decay, 2)
            act.wait_ge(s_const, 2)

            def mixer(g):
                act.wait_ge(pe_xnT, g + 1)
                ge(act, v_gated, g)
                ge(act, pe_z, g)
                act.copy(xnT[:], ps_xnT[:]).then_inc(a_xnT, 1)
                act.wait_ge(pe_z, g + 1)
                act.activation(ti[:], ps_zi[:], ACT.Tanh, bias=bias_i[:], scale=0.5)
                act.activation(tr[:], ps_zr[:], ACT.Tanh, bias=bias_r[:], scale=0.5).then_inc(l_act, 1)
                act.wait_ge(l_act, g * 2 + 3)
                ge(act, v_scan, g)
                act.activation(at[:], tr[:], ACT.Exp, bias=decay[:, 5:6], scale=decay[:, 5:6]).then_inc(a_at, 1)
                act.wait_ge(a_at, g + 1)
                act.activation(at2[:], at[:], ACT.Square).then_inc(l_act, 1)

            def std_first(g):
                act.wait_ge(v_var1, g + 1)
                act.activation(std1[:], mv1[:, :, 1], ACT.Sqrt, bias=eps_c[:]).then_inc(a_std1, 1)

            def root(g):
                act.wait_ge(l_act, g * 2 + 4)
                act.activation(bq[:], at2[:], ACT.Sqrt, bias=decay[:, 4:5], scale=-0.25).then_inc(a_gate, 1)

            def std_mixed(g):
                act.wait_ge(v_varh, g + 1)
                act.activation(stdh[:], mvh[:, :, 1], ACT.Sqrt, bias=eps_c[:]).then_inc(a_stdh, 1)

            def std_second(g):
                act.wait_ge(v_var2, g + 1)
                act.activation(std2[:], mv2[:, :, 1], ACT.Sqrt, bias=eps_c[:]).then_inc(a_std2, 1)

            def router(g):
                act.wait_ge(pe_x2T, g + 1)
                ge(act, pe_logit, g)
                act.copy(xn2T[:], ps_x2T[:]).then_inc(a_x2T, 1)
                act.copy(xn2_all[:, bass.ds(g * GT, GT), :], xn2[:]).then_inc(a_x2c, 1)
                act.wait_ge(pe_logit, g + 1)
                act.activation(th[:].rearrange("p j e -> p (j e)"), ps_logit[:, 0:GT * E], ACT.Tanh,
                               scale=0.5).then_inc(a_th, 1)

            def step(s, mix, nxt, old, route):
                if mix:
                    mixer(s)
                if nxt:
                    std_first(s + 1)
                if mix:
                    root(s)
                if old:
                    std_mixed(s - 1)
                if route:
                    std_second(s - 2)
                    router(s - 2)

            std_first(0)
            step(0, True, True, False, False)
            step(1, True, True, True, False)
            step(2, True, True, True, True)
            act.wait_ge(v_wscale, 1)
            act.activation(w13_h[:], w13_raw, ACT.Identity, scale=wscale[:, 0:1]).then_inc(a_wh, 1)
            act.activation(w2_h[:], w2_raw, ACT.Identity, scale=wscale[0:I, 1:2]).then_inc(a_wh, 1)
            with act.Fori(3, G - 1) as s:
                step(s, True, True, True, True)
            step(G - 1, True, False, True, True)
            step(G, False, False, True, True)
            step(G + 1, False, False, False, True)

            for h in range(HALVES):
                most = steps_value(act, h)
                if h:
                    wait_apart(act, b_y[h - 1], most_before * 2 + 6)
                most_before = most
                act.preload_act_table(ACT.Tanh)

                def slot(t, p, on):
                    o = 1 - p
                    if on[4]:
                        act.wait_ge(b_aT[h], t - 3)
                        if on[6]:
                            act.wait_ge(b_y[h], t - 5)
                        act.copy(aT[:, p, :, :, :].rearrange("i b f t -> i (b f t)"),
                                 ps_aT[p][0:I, :].bitcast(F16)[:, 0:4 * P]).then_inc(b_aTc[h], 1)
                    if on[0]:
                        act.wait_ge(b_xT[h], t + 1)
                        act.copy(xbT_h[:, p, :, :].rearrange("c b t -> c (b t)"), ps_xbT[p][:, 0:2 * P]).then_inc(b_xh[h], 1)
                    if on[2]:
                        act.wait_ge(b_act[h], t - 1)
                        act.copy(act_h[:, p, :, :], act_a[:, p, :, :]).then_inc(b_ah[h], 1)
                    if on[1]:
                        act.wait_ge(b_gu[h], t)
                        act.activation(act_t[:, o, :, :], ps_gu[o][:, 0:4 * I].rearrange(
                            "t (b w i) -> t b w i", b=2, w=2)[:, :, 0, :], ACT.Tanh, scale=wscale[:, 2:3]).then_inc(b_tanh[h], 1)

                for t in range(6):
                    slot(t, t % 2, stages(t))
                with act.Fori(1, most + 1) as q:
                    for p in range(2):
                        slot(q * 2 + 4 + p, p, stages())
                for t in range(4):
                    slot(most * 2 + 6 + t, t % 2, stages(left=t))

        @block.vector
        def _(dve):
            dve.wait_ge(s_small, 64)
            dve.memset(decay[:, 4:5], 0.25)
            dve.wait_ge(s_decay, 1)
            dve.scalar_tensor_tensor(out=decay[:, 5:6], in0=decay[:, 0:1], scalar=0.0, in1=decay[:, 3:4],
                                     op0=ALU.max, op1=ALU.add).then_inc(l_tab, 1)
            dve.wait_ge(l_tab, 1)
            dve.tensor_scalar(decay[:, 5:6], decay[:, 5:6], -4.0, None, ALU.mult).then_inc(s_decay, 1)
            dve.wait_ge(s_setT, 1)
            dve.tensor_copy(wiT[:], ps_setup[:, 0:P])
            dve.tensor_copy(wrT[:], ps_setup[:, P:2 * P])
            dve.tensor_copy(gateT[:], ps_setup[:, 2 * P:2 * P + E]).then_inc(s_wT, 1)
            dve.wait_ge(s_const, 2)

            def stats(source, st, mv, link, n):
                for j in range(GT):
                    ins = dve.bn_stats(st[:, j, :], source(j))
                ins.then_inc(link, 1)
                wait_apart(dve, link, n)
                for j in range(GT):
                    ins = dve.bn_aggr(mv[:, j, :], st[:, j, :])
                return ins

            def stats_first(g):
                wait_apart(dve, s_x, 16 * (g + 1))
                stats(lambda j: x_sb[:, bass.ds(g * GT + j, 1), :].rearrange("p a c -> p (a c)"),
                      st1, mv1, l_ln1, g * 2 + 1).then_inc(v_var1, 1)

            def norm_first(g):
                dve.wait_ge(a_std1, g + 1)
                dve.reciprocal(rstd1[:], std1[:]).then_inc(l_ln1, 1)
                dve.wait_ge(l_ln1, g * 2 + 2)
                ge(dve, pe_xnT, g)
                for j in range(GT):
                    ins = dve.tensor_scalar(xn[:, j, :], x_sb[:, bass.ds(g * GT + j, 1), :].rearrange("p a c -> p (a c)"),
                                            mv1[:, j, 0:1], rstd1[:, j:j + 1], ALU.subtract, ALU.mult)
                ins.then_inc(v_xn, 1)

            def recur(g):
                dve.wait_ge(a_gate, g + 1)
                dve.scalar_tensor_tensor(out=gated[:], in0=ti[:], scalar=1.0, in1=xnT[:],
                                         op0=ALU.add, op1=ALU.mult).then_inc(v_gated, 1)
                dve.wait_ge(v_gated, g + 1)
                dve.tensor_tensor(gx[:], bq[:], gated[:], ALU.mult).then_inc(l_scan, 1)
                dve.wait_ge(l_scan, g + 1)
                ge(dve, pe_h, g)
                for t in range(0, GC, SEQ):
                    ins = dve.tensor_tensor_scan(hT[:, t:t + SEQ], at[:, t:t + SEQ], gx[:, t:t + SEQ], 0.0,
                                                 ALU.mult, ALU.add)
                ins.then_inc(v_scan, 1)

            def stats_mixed(g):
                wait_apart(dve, pe_h, g + 1)
                stats(lambda j: ps_h[:, j * P:(j + 1) * P], sth, mvh, l_x1, g * 4 + 1).then_inc(v_varh, 1)

            def add_mixed(g):
                dve.wait_ge(a_stdh, g + 1)
                dve.reciprocal(rstdh[:], stdh[:]).then_inc(l_x1, 1)
                dve.wait_ge(l_x1, g * 4 + 2)
                for j in range(GT):
                    ins = dve.tensor_scalar(hn[:, j, :], ps_h[:, j * P:(j + 1) * P],
                                            mvh[:, j, 0:1], rstdh[:, j:j + 1], ALU.subtract, ALU.mult)
                ins.then_inc(l_x1, 1)
                dve.wait_ge(l_x1, g * 4 + 3)
                dve.tensor_tensor(x_sb[:, bass.ds(g * GT, GT), :], x_sb[:, bass.ds(g * GT, GT), :], hn[:],
                                  ALU.add).then_inc(v_x1, 1)
                wait_apart(dve, v_x1, g + 1)
                stats(lambda j: x_sb[:, bass.ds(g * GT + j, 1), :].rearrange("p a c -> p (a c)"),
                      st2, mv2, l_x1, g * 4 + 4).then_inc(v_var2, 1)

            def norm_second(g):
                dve.wait_ge(a_std2, g + 1)
                dve.reciprocal(rstd2[:], std2[:]).then_inc(l_route, 1)
                dve.wait_ge(l_route, g * DVE_ROUTE + 1)
                ge(dve, pe_x2T, g)
                ge(dve, a_x2c, g)
                for j in range(GT):
                    ins = dve.tensor_scalar(xn2[:, j, :], x_sb[:, bass.ds(g * GT + j, 1), :].rearrange("p a c -> p (a c)"),
                                            mv2[:, j, 0:1], rstd2[:, j:j + 1], ALU.subtract, ALU.mult)
                ins.then_inc(v_xn2, 1)

            def route(g):
                n = [1]

                def link(ins):
                    n[0] += 1
                    ins.then_inc(l_route, 1)
                    wait_apart(dve, l_route, g * DVE_ROUTE + n[0])

                dve.wait_ge(a_th, g + 1)
                link(dve.tensor_scalar(score[:], th[:], 0.5, 0.5, ALU.mult, ALU.add))
                link(dve.tensor_tensor(biased[:], score[:], ebias[:].unsqueeze(1).to_broadcast([P, GT, E]), ALU.add))
                for j in range(GT):
                    ins = dve.max(top[:, j, :], biased[:, j, :])
                link(ins)
                for j in range(GT):
                    ins = dve.max_index(top_i[:, j, :], top[:, j, :], biased[:, j, :])
                link(ins)
                link(dve.tensor_copy(top_f[:], top_i[:, :, 0:K]))
                hot = hot_all[:, bass.ds(g * GT, GT), :, :]
                link(dve.tensor_tensor(hot, iota_e[:].unsqueeze(1).unsqueeze(1).to_broadcast([P, GT, K, E]),
                                       top_f[:].unsqueeze(3).to_broadcast([P, GT, K, E]), ALU.is_equal))
                with nc.allow_low_precision(reason="a mask of zeros and ones"):
                    dve.tensor_reduce(mask[:], hot.rearrange("p j k e -> p j e k"), AX_X, ALU.add).then_inc(v_mask, 1)
                link(dve.tensor_tensor(picked[:], hot, score[:].unsqueeze(2).to_broadcast([P, GT, K, E]), ALU.mult))
                link(dve.tensor_reduce(wsel[:], picked[:], AX_X, ALU.add))
                link(dve.tensor_reduce(wsum[:], wsel[:], AX_X, ALU.add))
                link(dve.reciprocal(winv[:], wsum[:]))
                dve.tensor_tensor(wt_all[:, bass.ds(g * GT, GT), :], wsel[:],
                                  winv[:].unsqueeze(2).to_broadcast([P, GT, K]), ALU.mult).then_inc(v_wt, 1)
                dve.wait_ge(pe_pos, g + 1)
                link(dve.tensor_tensor(pos[:], ps_pos[:, 0:GT * E].rearrange("p (j e) -> p j e", j=GT),
                                       region_e[:].unsqueeze(1).to_broadcast([P, GT, E]), ALU.add))
                link(dve.tensor_tensor(picked[:], hot, pos[:].unsqueeze(2).to_broadcast([P, GT, K, E]), ALU.mult))
                rows = row_f[:, bass.ds(g * GT, GT), :]
                link(dve.tensor_reduce(rows, picked[:], AX_X, ALU.add))
                dve.tensor_copy(row_xs[:, bass.ds(g * GT * K, GT * K)].rearrange("p (j k) -> p j k", j=GT),
                                rows).then_inc(v_row, 1)
                link(dve.tensor_reduce(add4[:], mask[:].rearrange("p j e -> p e j"), AX_X, ALU.add))
                with nc.allow_low_precision(reason="counts of at most 16"):
                    dve.tensor_tensor(seen[:], seen[:], add4[:], ALU.add).then_inc(v_seen, 1)
                assert n[0] == DVE_ROUTE

            def tables(h):
                n = [h * DVE_TABLES + 1]

                def link(ins):
                    n[0] += 1
                    ins.then_inc(l_tab, 1)
                    dve.wait_ge(l_tab, n[0])

                dve.wait_ge(pe_cnt, h + 1)
                link(dve.tensor_copy(cnt[:], ps_pos[:, 128:128 + E]))
                if h + 1 < HALVES:
                    dve.wait_ge(v_seen, (h + 1) * GH)
                    dve.memset(seen[:], 0.0).then_inc(v_seen, 1)
                link(dve.tensor_scalar(cnt_up[:], cnt[:], float(P - 1), None, ALU.add))
                link(dve.tensor_scalar(nblk_i[:], cnt_up[:], 7, None, ALU.logical_shift_right))
                link(dve.tensor_copy(nblk[:], nblk_i[:]))
                link(dve.tensor_tensor_scan(cum[:], ones_e[:], nblk[:], 0.0, ALU.mult, ALU.add))
                link(dve.tensor_scalar(past[:], cum[:], iota_p[:], None, ALU.is_le))
                link(dve.tensor_tensor(past_n[:], past[:], nblk[:], ALU.mult))
                link(dve.tensor_reduce(tcol[:, 0:1], past[:], AX_X, ALU.add))
                link(dve.tensor_reduce(tcol[:, 1:2], past_n[:], AX_X, ALU.add))
                link(dve.tensor_scalar(tcol[:, 2:3], tcol[:, 0:1], float(E - 1), None, ALU.min))
                link(dve.tensor_tensor(tcol[:, 3:4], iota_p[:], tcol[:, 1:2], ALU.subtract))
                link(dve.tensor_scalar(tcol[:, 4:5], tcol[:, 3:4], float(P), None, ALU.mult))
                link(dve.scalar_tensor_tensor(out=tcol[:, 5:6], in0=tcol[:, 0:1], scalar=float(REGION), in1=tcol[:, 4:5],
                                              op0=ALU.mult, op1=ALU.add))
                dve.tensor_tensor(past_n[:], cnt[:], region_e[:], ALU.add).then_inc(v_tcol, 1)
                link(dve.tensor_scalar(steps_u[:, 0:1], cum[0:1, E - 1:E], -1.0 - 2.0 * SLOTS, None, ALU.add))
                link(dve.tensor_scalar(steps_of[h][:], steps_u[:, 0:1], SLOTS.bit_length() - 1, None, ALU.logical_shift_right))
                dve.wait_ge(v_tcol, h + 1)
                dve.tensor_copy(tail_of[h][:], past_n[0:1, :])
                dve.wait_ge(pe_tab, h + 1)
                link(dve.tensor_copy(expert_of[h][:], ps_setup[0:1, 0:P]))
                dve.tensor_copy(row_of[h][:], ps_setup[0:1, P:2 * P]).then_inc(v_tab, 1)
                link(dve.tensor_tensor(past[:], cum[:], nblk[:], ALU.subtract))
                link(dve.scalar_tensor_tensor(out=pack[:], in0=past[:], scalar=float(P), in1=region_e[:],
                                              op0=ALU.mult, op1=ALU.subtract))
                for g in range(h * GH, (h + 1) * GH):
                    link(dve.tensor_tensor(picked[:], hot_all[:, g * GT:(g + 1) * GT, :, :],
                                           pack[:].unsqueeze(1).unsqueeze(1).to_broadcast([P, GT, K, E]), ALU.mult))
                    link(dve.tensor_reduce(wsel[:], picked[:], AX_X, ALU.add))
                    dve.tensor_tensor(row_ys[:, g * GT * K:(g + 1) * GT * K].rearrange("p (j k) -> p j k", j=GT),
                                      row_f[:, g * GT:(g + 1) * GT, :], wsel[:], ALU.add).then_inc(v_pack, 1)
                assert n[0] == (h + 1) * DVE_TABLES + 1

            def step(s, mix, nxt, old, rt):
                if mix:
                    norm_first(s)
                if old:
                    stats_mixed(s - 1)
                if nxt:
                    stats_first(s + 1)
                if rt:
                    norm_second(s - 2)
                if old:
                    add_mixed(s - 1)
                if mix:
                    recur(s)
                if rt:
                    route(s - 2)

            def weights_max():
                dve.wait_ge(s_wexp, 48)
                dve.tensor_reduce(wmax[:, 0:1], w13_raw.rearrange("c e w i -> c (e w i)"), AX_X, ALU.max, apply_absolute_value=True)
                dve.tensor_reduce(wmax[0:I, 1:2], w2_raw.rearrange("i e c -> i (e c)"), AX_X, ALU.max,
                                  apply_absolute_value=True).then_inc(v_wmax, 1)

            def weights_scale():
                n = [0]

                def link(ins):
                    n[0] += 1
                    ins.then_inc(v_wrow, 1)
                    dve.wait_ge(v_wrow, n[0])

                dve.wait_ge(pe_wmax, 1)
                link(dve.tensor_reduce(wtop[:], ps_setup[0:1, 0:2 * P].rearrange("a (w p) -> a w p", w=2), AX_X, ALU.max))
                link(dve.tensor_scalar(wtop[:], wtop[:], 2.0 ** -60, None, ALU.max))
                link(dve.tensor_scalar(wpow[:].bitcast(U32), wtop[:].bitcast(U32), 0x7F800000, None, ALU.bitwise_and))
                link(dve.tensor_scalar(wrow[:, 4:6], wpow[:], 2.0, None, ALU.mult))
                link(dve.reciprocal(wrow[:, 0:2], wrow[:, 4:6]))
                link(dve.tensor_copy(wrow[:, 2:3], wpow[:, 0:1]))
                link(dve.tensor_tensor(wrow[:, 6:7], wrow[:, 4:5], wrow[:, 4:5], ALU.mult))
                link(dve.tensor_tensor(wrow[:, 3:4], wrow[:, 6:7], wpow[:, 1:2], ALU.mult))
                dve.wait_ge(pe_wrow, 1)
                dve.tensor_copy(wscale[:, 0:4], ps_setup[:, 0:4]).then_inc(v_wscale, 1)

            def weights_rest():
                dve.wait_ge(v_wscale, 1)
                for part, (lo, hi, raw) in enumerate(((w13_l[:], w13_h[:], w13_raw), (w2_l[:], w2_h[:], w2_raw))):
                    dve.wait_ge(a_wh, part + 1)
                    rows = raw.shape[0]
                    ins = dve.scalar_tensor_tensor(out=lo, in0=raw, scalar=wscale[0:rows, part:part + 1], in1=hi,
                                                   op0=ALU.mult, op1=ALU.subtract)
                ins.then_inc(v_wl, 1)

            dve.tensor_copy(ident_h[:], ident[:]).then_inc(s_wT, 1)
            stats_first(0)
            step(0, True, True, False, False)
            step(1, True, True, True, False)
            weights_max()
            step(2, True, True, True, True)
            weights_scale()
            weights_rest()
            with dve.Fori(3, GH + 2) as s:
                step(s, True, True, True, True)
            tables(0)
            with dve.Fori(GH + 2, G - 1) as s:
                step(s, True, True, True, True)
            step(G - 1, True, False, True, True)
            step(G, False, False, True, True)
            step(G + 1, False, False, False, True)
            tables(1)

            for h in range(HALVES):
                most = steps_value(dve, h)
                if h:
                    for p in range(2):
                        wait_apart(dve, s_ys[0][p], most_before * 16 + 48)
                most_before = most

                def slot(t, q, p, on):
                    gu = ps_gu[p][:, 0:4 * I].rearrange("t (b w i) -> t b w i", b=2, w=2)
                    if on[2]:
                        dve.wait_ge(b_tanh[h], t - 1)
                        dve.scalar_tensor_tensor(out=silu2[:, p, :, :], in0=act_t[:, p, :, :], scalar=1.0,
                                                 in1=gu[:, :, 0, :], op0=ALU.add, op1=ALU.mult).then_inc(b_silu[h], 1)
                        dve.wait_ge(b_silu[h], t - 1)
                        if on[4]:
                            dve.wait_ge(b_al[h], t - 3)
                        dve.tensor_tensor(act_a[:, p, :, :], silu2[:, p, :, :], gu[:, :, 1, :], ALU.mult).then_inc(b_act[h], 1)
                    if on[0]:
                        dve.wait_ge(b_xh[h], t + 1)
                        dve.tensor_tensor(xbT_l[:, p, :, :].rearrange("c b t -> c (b t)"), ps_xbT[p][:, 0:2 * P],
                                          xbT_h[:, p, :, :].rearrange("c b t -> c (b t)"), ALU.subtract).then_inc(b_xl[h], 1)
                    if on[2]:
                        dve.wait_ge(b_ah[h], t - 1)
                        dve.tensor_tensor(act_l[:, p, :, :], act_a[:, p, :, :], act_h[:, p, :, :], ALU.subtract).then_inc(b_al[h], 1)
                    if on[4]:
                        dve.wait_ge(b_y[h], t - 3)
                        if on[6]:
                            dve.wait_ge(s_ys[h][p], q * 16)
                        dve.tensor_copy(yb[:, p, :, :].rearrange("t b c -> t (b c)"), ps_y[p][:, 0:2 * P]).then_inc(b_yc[h], 1)

                for t in range(6):
                    slot(t, t // 2 - 2, t % 2, stages(t))
                with dve.Fori(1, most + 1) as q:
                    for p in range(2):
                        slot(q * 2 + 4 + p, q, p, stages())
                for t in range(4):
                    slot(most * 2 + 6 + t, most + 1 + t // 2, t % 2, stages(left=t))

            def combine(g, h):
                b = g % 2
                n = [g * 6]

                def link(ins):
                    n[0] += 1
                    ins.then_inc(l_mix, 1)
                    dve.wait_ge(l_mix, n[0])

                if g >= 2:
                    dve.wait_ge(c_fin, g - 1)
                dve.wait_ge(s_yk[b], 16 * GT * K * (g // 2 + 1))
                for k in range(K):
                    for j in range(GT):
                        t = g * GT + j
                        y = yk[h][:, t - h * TH, k, :]
                        if k == 0:
                            ins = dve.tensor_scalar(mix[:, b, j, :], y, wt_all[:, t, 0:1], None, ALU.mult)
                        else:
                            ins = dve.scalar_tensor_tensor(out=mix[:, b, j, :], in0=y, scalar=wt_all[:, t, k:k + 1],
                                                           in1=mix[:, b, j, :], op0=ALU.mult, op1=ALU.add)
                    link(ins)
                stats(lambda j: mix[:, b, j, :], st3, mv3[:, b, :, :], l_mix, n[0] + 1).then_inc(l_mix, 1)
                n[0] += 2
                dve.wait_ge(l_mix, n[0])
                dve.tensor_scalar(ve3[:, b, :], mv3[:, b, :, 1], EPS, None, ALU.add).then_inc(c_ve, 1)

            def finish(g):
                b = g % 2
                dve.wait_ge(c_pow, g + 1)
                for j in range(GT):
                    dve.tensor_scalar(mix[:, b, j, :], mix[:, b, j, :], mv3[:, b, j, 0:1], rstd3[:, b, j:j + 1],
                                      ALU.subtract, ALU.mult).then_inc(s_fin, 1)
                dve.wait_ge(s_fin, GT * (g + 1))
                dve.tensor_tensor(x_sb[:, g * GT:(g + 1) * GT, :], mix[:, b, :, :], x_sb[:, g * GT:(g + 1) * GT, :],
                                  ALU.add).then_inc(c_fin, 1)

            dve.tensor_scalar(wt_all[:], wt_all[:], wscale[:, 3:4], None, ALU.mult).then_inc(v_wt, 1)
            dve.wait_ge(v_wt, G + 1)
            for g in range(G):
                combine(g, g // GH)
                if g:
                    finish(g - 1)
            finish(G - 1)

        @block.tensor
        def _(pe):
            pe.wait_ge(s_const, 2)
            pe.wait_ge(s_wmix, 48)
            pe.transpose(ps_setup[:, 0:P], wi_raw[:], ident[:])
            pe.transpose(ps_setup[:, P:2 * P], wr_raw[:], ident[:])
            pe.transpose(ps_setup[:, 2 * P:2 * P + E], gate_raw[:], ident[0:E, 0:E]).then_inc(s_setT, 1)
            pe.wait_ge(s_wT, 2)

            def mixer(g):
                pe.wait_ge(v_xn, g + 1)
                ge(pe, a_xnT, g)
                for j in range(GT):
                    ins = pe.transpose(ps_xnT[:, j * P:(j + 1) * P], xn[:, j, :], ident[:])
                ins.then_inc(pe_xnT, 1)
                pe.wait_ge(a_xnT, g + 1)
                pe.matmul(ps_zi[:], wiT[:], xnT[:], start=True, stop=True)
                pe.matmul(ps_zr[:], wrT[:], xnT[:], start=True, stop=True).then_inc(pe_z, 1)

            def mixed(g):
                pe.wait_ge(v_scan, g + 1)
                for j in range(GT):
                    ins = pe.transpose(ps_h[:, j * P:(j + 1) * P], hT[:, j * P:(j + 1) * P], ident[:])
                ins.then_inc(pe_h, 1)

            def router(g):
                pe.wait_ge(v_xn2, g + 1)
                ge(pe, a_x2T, g)
                for j in range(GT):
                    ins = pe.transpose(ps_x2T[:, j * P:(j + 1) * P], xn2[:, j, :], ident[:])
                ins.then_inc(pe_x2T, 1)
                pe.wait_ge(a_x2T, g + 1)
                for j in range(GT):
                    ins = pe.matmul(ps_logit[:, j * E:(j + 1) * E], xn2T[:, j * P:(j + 1) * P], gateT[:],
                                    start=True, stop=True)
                ins.then_inc(pe_logit, 1)

            def positions(g, reset):
                pe.wait_ge(v_mask, g + 1)
                ge(pe, v_seen, g + reset)
                for j in range(GT):
                    dst = ps_pos[:, j * E:(j + 1) * E]
                    pe.matmul(dst, ones[:], seen[:], start=True, stop=False)
                    for i in range(j):
                        pe.matmul(dst, ones[:], mask[:, i, :], start=False, stop=False)
                    ins = pe.matmul(dst, before[:], mask[:, j, :], start=False, stop=True)
                ins.then_inc(pe_pos, 1)

            def tables(h):
                pe.wait_ge(v_seen, (h + 1) * GH + h)
                pe.matmul(ps_pos[:, 128:128 + E], ones[:], seen[:], start=True, stop=True).then_inc(pe_cnt, 1)
                pe.wait_ge(v_tcol, h + 1)
                pe.transpose(ps_setup[0:1, 0:P], tcol[:, 2:3], ident[:])
                pe.transpose(ps_setup[0:1, P:2 * P], tcol[:, 5:6], ident[:]).then_inc(pe_tab, 1)

            def step(s, mix, rt, reset=0):
                if mix:
                    mixer(s)
                if rt:
                    router(s - 2)
                if mix:
                    mixed(s)
                if rt:
                    positions(s - 2, reset)

            step(0, True, False)
            step(1, True, False)
            pe.wait_ge(v_wmax, 1)
            pe.transpose(ps_setup[0:1, 0:P], wmax[:, 0:1], ident[:])
            pe.transpose(ps_setup[0:1, P:2 * P], wmax[:, 1:2], ident[:]).then_inc(pe_wmax, 1)
            step(2, True, True)
            pe.wait_ge(v_wrow, 8)
            pe.matmul(ps_setup[:, 0:4], ones_row[:], wrow[:, 0:4], start=True, stop=True).then_inc(pe_wrow, 1)
            with pe.Fori(3, GH + 2) as s:
                step(s, True, True)
            tables(0)
            with pe.Fori(GH + 2, G) as s:
                step(s, True, True, 1)
            step(G, False, True, 1)
            step(G + 1, False, True, 1)
            tables(1)

            pe.wait_ge(v_wl, 1)
            back_experts, gu_experts = rows_loader(pe, "expert_y", 4), rows_loader(pe, "expert_gu", 4)
            for h in range(HALVES):
                most = steps_value(pe, h)
                if h:
                    wait_apart(pe, b_yc[h - 1], most_before * 2 + 6)
                most_before = most

                def slot(t, q, p, on, e_gu, e_y):
                    o = 1 - p
                    if on[0]:
                        for b in range(2):
                            pe.wait_ge(s_xb[h][2 * p + b], q * 16 + 48)
                            ins = pe.transpose(ps_xbT[p][:, b * P:(b + 1) * P], xb[:, 2 * p + b, :], ident[:])
                        ins.then_inc(b_xT[h], 1)
                    if on[1]:
                        pe.wait_ge(b_xl[h], t)
                        if on[3]:
                            pe.wait_ge(b_act[h], t - 2)
                        for b in range(2):
                            dst = ps_gu[o][:, b * 2 * I:(b + 1) * 2 * I]
                            w_h, w_l = (w[:, bass.ds(e_gu[b], 1), :, :].rearrange("c a w i -> c (a w i)")
                                        for w in (w13_h, w13_l))
                            pe.matmul(dst, xbT_h[:, o, b, :], w_h, start=True, stop=False)
                            pe.matmul(dst, xbT_h[:, o, b, :], w_l, start=False, stop=False)
                            ins = pe.matmul(dst, xbT_l[:, o, b, :], w_h, start=False, stop=True)
                        ins.then_inc(b_gu[h], 1)
                    if on[4]:
                        pe.wait_ge(b_aTc[h], t - 3)
                        if on[6]:
                            pe.wait_ge(b_yc[h], t - 5)
                        for b in range(2):
                            dst = ps_y[p][:, b * P:(b + 1) * P]
                            w_h, w_l = (w[:, bass.ds(e_y[b], 1), :].rearrange("i a c -> i (a c)") for w in (w2_h, w2_l))
                            pe.matmul(dst, aT[:, p, b, 0, :], w_h, start=True, stop=False)
                            pe.matmul(dst, aT[:, p, b, 0, :], w_l, start=False, stop=False)
                            ins = pe.matmul(dst, aT[:, p, b, 1, :], w_h, start=False, stop=True)
                        ins.then_inc(b_y[h], 1)
                    if on[3]:
                        pe.wait_ge(b_al[h], t - 2)
                        aT16 = ps_aT[o][0:I, :].bitcast(F16)
                        for b in range(2):
                            for f, part in enumerate((act_h, act_l)):
                                at16 = (2 * b + f) * P
                                ins = pe.transpose(aT16[:, at16:at16 + P], part[:, o, b, :], ident_h[:])
                        ins.then_inc(b_aT[h], 1)

                def step(t, q, on0, on1):
                    e_y = back_experts(expert_of[h], q * SLOTS, E - 1) if on1[4] else [None] * 4
                    at = 0 if isinstance(q, int) and q == -2 else q * SLOTS + 6
                    e_gu = gu_experts(expert_of[h], at, E - 1)
                    if isinstance(q, int) and q == -2:
                        e_gu = [None] * 2 + e_gu[0:2]
                    slot(t, q, 0, on0, e_gu[0:2], e_y[0:2])
                    slot(t + 1, q, 1, on1, e_gu[2:4], e_y[2:4])

                for t in (0, 2, 4):
                    step(t, t // 2 - 2, stages(t), stages(t + 1))
                with pe.Fori(1, most + 1) as q:
                    step(q * 2 + 4, q, stages(), stages())
                for t in (0, 2):
                    step(most * 2 + 6 + t, most + 1 + t // 2, stages(left=t), stages(left=t + 1))


_INS = ["L0_attn_x", "L0_attn_Wi", "L0_attn_bi", "L0_attn_Wr", "L0_attn_br", "L0_attn_cap_lambda",
        "L0_ffn_gate_w", "L0_ffn_w1", "L0_ffn_w3", "L0_ffn_w2", "L0_ffn_e_bias"]


def kernel(**inputs):
    import numpy as _np
    import concourse.bacc as _bacc
    from concourse import mybir as _mybir
    from concourse.bass_utils import run_bass_kernel_spmd as _run

    nc = _bacc.Bacc("TRN2", target_bir_lowering=False, num_devices=1)
    arrays, args = {}, []
    for name in _INS:
        a = _np.ascontiguousarray(inputs[name])
        arrays[f"in_{name}_dram"] = a
        args.append(nc.dram_tensor(f"in_{name}_dram", a.shape, _mybir.dt.from_np(a.dtype), kind="ExternalInput").ap())
    shape = inputs["L0_attn_x"].shape
    experts = inputs["L0_ffn_gate_w"].shape[0]
    fp32 = _mybir.dt.float32
    args.append(nc.dram_tensor("out_0_dram", shape, fp32, kind="ExternalOutput").ap())
    tokens = shape[0] * shape[1] // HALVES
    blocks = -(-(tokens * K // P + experts - 1) // SLOTS) * SLOTS
    for kind, rows in (("xs", (experts + 1) * (tokens + P)), ("ys", blocks * P)):
        args.append([nc.dram_tensor(f"{kind}{h}_dram", (rows, shape[2]), fp32, kind="Internal").ap() for h in range(HALVES)])
    sandwich_kernel(nc, *args)
    r = _run(nc, [arrays], core_ids=[0])
    return r.results[0]["out_0_dram"]
```

```python
from contextlib import ExitStack

import concourse.bass as bass
from concourse import mybir

ALU = mybir.AluOpType
ACT = mybir.ActivationFunctionType
AX_X, AX_XY = mybir.AxisListType.X, mybir.AxisListType.XY
F32 = mybir.dt.float32
BF16 = mybir.dt.bfloat16
F16 = mybir.dt.float16
U32 = mybir.dt.uint32
I32 = mybir.dt.int32

P = 128
EPS = 1e-5
K = 4
GT = 4
HALVES = 2
SLOTS = 4
DVE_TABLES = 17


def sandwich_kernel(nc: bass.Bass, x, Wi, bi, Wr, br, cap, gate_w, w1, w3, w2, e_bias, out, xs, ys):
    B, T, C = x.shape
    E, _, I = w1.shape
    TILES = B * T // P
    G = TILES // GT
    GH = G // HALVES
    TH = TILES // HALVES
    GC = GT * P
    SEQ = T
    REGION = TH * P + P
    MAX_BLOCKS = ys[0].shape[0] // P
    assert C == P and GC % SEQ == 0

    x_rows = x.rearrange("b t c -> (b t) c").rearrange("(n p) c -> p n c", p=P)
    out_rows = out.rearrange("b t c -> (b t) c").rearrange("(n p) c -> p n c", p=P)

    with ExitStack() as ctx:
        def sb(name, shape, dt=F32):
            return ctx.enter_context(nc.sbuf_tensor(name, shape, dt))

        def sem(name):
            return ctx.enter_context(nc.semaphore(name))

        bank = [ctx.enter_context(nc.psum_tensor(f"bank{i}", [P, 512], F32)) for i in range(8)]
        ps_xnT, ps_zi, ps_zr, ps_h, ps_x2T, ps_logit, ps_pos = bank[:7]
        ps_setup = bank[7]
        ps_xbT, ps_gu, ps_aT, ps_y = (bank[2 * i:2 * i + 2] for i in range(4))

        wi_raw, wr_raw, gate_raw = sb("wi_raw", [P, C]), sb("wr_raw", [P, C]), sb("gate_raw", [E, C])
        wiT, wrT, gateT = sb("wiT", [C, P]), sb("wrT", [C, P]), sb("gateT", [C, E])
        w13, w2s = sb("w13", [C, E, 2, 2, I], F16), sb("w2s", [I, E, 2, C], F16)
        w13_h, w13_l, w2_h, w2_l = w13[:, :, 0, :, :], w13[:, :, 1, :, :], w2s[:, :, 0, :], w2s[:, :, 1, :]
        wmax, wtop3 = sb("wmax", [P, 3]), sb("wtop3", [1, 3])
        wtop, wpow, wrow, wscale = sb("wtop", [1, 2]), sb("wpow", [1, 2]), sb("wrow", [1, 8]), sb("wscale", [P, 8])
        ones_row = sb("ones_row", [1, P])
        ident_h = sb("ident_h", [P, P], F16)
        bias_i, bias_r, decay = sb("bias_i", [P, 1]), sb("bias_r", [P, 1]), sb("decay", [P, 6])
        ebias = sb("ebias", [P, E])
        ident = sb("ident", [P, P])
        before = sb("before", [P, P], BF16)
        ones = sb("ones", [P, P], BF16)
        iota_e, region_e, iota_p = sb("iota_e", [P, E]), sb("region_e", [P, E]), sb("iota_p", [P, 1])
        eps_c = sb("eps_c", [P, 1])
        zeros = sb("zeros", [P, P])

        x_sb = sb("x_sb", [P, TILES, C])
        xn2_all = sb("xn2_all", [P, TILES, C])
        row_xs, row_ys = sb("row_xs", [P, TILES * K], U32), sb("row_ys", [P, TILES * K], U32)
        row_f = sb("row_f", [P, TILES, K])
        wt_all = sb("wt_all", [P, TILES, K])

        st1, mv1, std1 = sb("st1", [P, GT, 6]), sb("mv1", [P, GT, 2]), sb("std1", [P, GT])
        shift1, shifth, shift2 = (sb(n, [P, GT]) for n in ("shift1", "shifth", "shift2"))
        rstd1, xn, xnT = sb("rstd1", [P, GT]), sb("xn", [P, GT, C]), sb("xnT", [C, GC])
        ti, tr, at, at2, bq = (sb(n, [P, GC]) for n in ("ti", "tr", "at", "at2", "bq"))
        gated, gx, hT = sb("gated", [P, GC]), sb("gx", [P, GC]), sb("hT", [P, GC])
        sth, mvh, stdh = sb("sth", [P, GT, 6]), sb("mvh", [P, GT, 2]), sb("stdh", [P, GT])
        rstdh, hn = sb("rstdh", [P, GT]), sb("hn", [P, GT, C])
        st2, mv2, std2 = sb("st2", [P, GT, 6]), sb("mv2", [P, GT, 2]), sb("std2", [P, GT])
        rstd2, xn2, xn2T = sb("rstd2", [P, GT]), sb("xn2", [P, GT, C]), sb("xn2T", [C, GC])
        th_all, ebias_half, biased = sb("th_all", [P, TILES, E]), sb("ebias_half", [P, E]), sb("biased", [P, GT, E])
        top, top_i, top_f = sb("top", [P, GT, 8]), sb("top_i", [P, GT, 8], U32), sb("top_f", [P, GT, K])
        hot_all, picked = sb("hot_all", [P, TILES, K, E], BF16), sb("picked", [P, GT, K, E])
        mask, seen, add4 = sb("mask", [P, GT, E], BF16), sb("seen", [P, E], BF16), sb("add4", [P, E])
        pos = sb("pos", [P, GT, E])
        wscore = sb("wscore", [P, GT, K])
        wsel, wsum, winv = sb("wsel", [P, GT, K]), sb("wsum", [P, GT]), sb("winv", [P, GT])

        cnt, cnt_up, nblk_i, nblk = sb("cnt", [P, E]), sb("cnt_up", [P, E], I32), sb("nblk_i", [P, E], I32), sb("nblk", [P, E])
        pack = [sb(f"pack{h}", [P, E]) for h in range(HALVES)]
        shift_f = sb("shift_f", [P, GT, K])
        cum, past, past_n = sb("cum", [P, E]), sb("past", [P, E]), sb("past_n", [P, E])
        ones_e = sb("ones_e", [P, E])
        tcol = sb("tcol", [P, 8])
        steps_f, steps_u = sb("steps_f", [1, 2]), sb("steps_u", [1, 2], I32)
        expert_of = [sb(f"expert_of{h}", [1, P], I32) for h in range(HALVES)]
        row_of = [sb(f"row_of{h}", [1, P], I32) for h in range(HALVES)]
        tail_of = [sb(f"tail_of{h}", [1, E], I32) for h in range(HALVES)]
        steps_of = [sb(f"steps_of{h}", [1, 1], I32) for h in range(HALVES)]

        xb = sb("xb", [P, SLOTS, C])
        xbT_h, xbT_l = sb("xbT_h", [C, 2, 2, P], F16), sb("xbT_l", [C, 2, 2, P], F16)
        act_t, silu2, act_a = (sb(n, [P, 2, 2, I]) for n in ("act_t", "silu2", "act_a"))
        act_h, act_l = sb("act_h", [P, 2, 2, I], F16), sb("act_l", [P, 2, 2, I], F16)
        aT, yb = sb("aT", [I, 2, 2, 2, P], F16), sb("yb", [P, 2, 2, C])

        y2 = gated[:].rearrange("p (q b c) -> p q b c", q=2, b=2)

        yk = [sb(f"yk{h}", [P, TH, K, C]) for h in range(HALVES)]
        w13_raw = yk[1][:].rearrange("p t k c -> p (t k c)")[:, 0:E * 2 * I].rearrange("p (e w i) -> p e w i", e=E, w=2)
        w2_raw = yk[0][:].rearrange("p t k c -> p (t k c)")[0:I, 0:E * C].rearrange("p (e c) -> p e c", e=E)
        mix = [sb("mix", [P, GT, C]), xn, xn2]
        shifts = mix[0][:].rearrange("p j (k e) -> p j k e", k=K)
        st3, mv3, std3, rstd3 = sb("st3", [P, GT, 6]), sb("mv3", [P, 2, GT, 2]), sb("std3", [P, 2, GT]), sb("rstd3", [P, 2, GT])
        shift3 = sb("shift3", [P, 2, GT])

        s_wmix, s_small, s_x = sem("s_wmix"), sem("s_small"), sem("s_x")
        s_wexp = [sem(f"s_wexp{i}") for i in (1, 3, 2)]
        v_ebias = sem("v_ebias")
        s_const, s_z0, s_setT, s_wT, s_bias, s_decay = (sem(n) for n in (
            "s_const", "s_z0", "s_setT", "s_wT", "s_bias", "s_decay"))
        v_var1, a_std1, v_rstd1, v_shift1, a_xn, pe_xnT, a_xnT, pe_zi, pe_z, a_t, a_at, a_at2, a_gate = (sem(n) for n in (
            "v_var1", "a_std1", "v_rstd1", "v_shift1", "a_xn", "pe_xnT", "a_xnT", "pe_zi", "pe_z", "a_t", "a_at", "a_at2", "a_gate"))
        v_gated, v_gx, v_scan, pe_h = (sem(n) for n in ("v_gated", "v_gx", "v_scan", "pe_h"))
        v_sth, v_varh, a_stdh, v_rstdh, v_shifth, a_hn, v_x1, v_st2, v_var2, a_std2, v_st1 = (sem(n) for n in (
            "v_sth", "v_varh", "a_stdh", "v_rstdh", "v_shifth", "a_hn", "v_x1", "v_st2", "v_var2", "a_std2", "v_st1"))
        v_rstd2, v_shift2, a_xn2, pe_x2T, a_x2T, a_x2c, pe_logit, a_th = (sem(n) for n in (
            "v_rstd2", "v_shift2", "a_xn2", "pe_x2T", "a_x2T", "a_x2c", "pe_logit", "a_th"))
        v_biased, v_top, v_top_i, v_top_f, v_hot, v_mask, v_add4, v_seen = (sem(n) for n in (
            "v_biased", "v_top", "v_top_i", "v_top_f", "v_hot", "v_mask", "v_add4", "v_seen"))
        v_chosen, v_wsel, v_wscore, v_wsum, v_winv, v_wt = (sem(n) for n in (
            "v_chosen", "v_wsel", "v_wscore", "v_wsum", "v_winv", "v_wt"))
        pe_pos, v_pos, v_picked, v_rowf, v_row = (sem(n) for n in ("pe_pos", "v_pos", "v_picked", "v_rowf", "v_row"))
        l_act, l_tab, l_mix = (sem(n) for n in ("l_act", "l_tab", "l_mix"))
        s_scat = [sem(f"s_scat{h}") for h in range(HALVES)]
        v_shift, l_pack, v_pack = sem("v_shift"), sem("l_pack"), sem("v_pack")
        pe_cnt, v_tcol, pe_tab, v_tab = sem("pe_cnt"), sem("v_tcol"), sem("pe_tab"), sem("v_tab")
        s_fill = [sem(f"s_fill{h}") for h in range(HALVES)]
        s_tail = [sem(f"s_tail{h}") for h in range(HALVES)]
        s_xb = [[sem(f"s_xb{h}_{u}") for u in range(SLOTS)] for h in range(HALVES)]
        s_ys = [[sem(f"s_ys{h}_{p}") for p in range(2)] for h in range(HALVES)]
        b_xT, b_xh, b_xl, b_gu, b_tanh, b_silu, b_act, b_ah, b_al, b_aT, b_aTc, b_y, b_y2, b_yc = (
            [sem(f"{n}{h}") for h in range(HALVES)] for n in (
                "b_xT", "b_xh", "b_xl", "b_gu", "b_tanh", "b_silu", "b_act", "b_ah", "b_al", "b_aT", "b_aTc", "b_y", "b_y2", "b_yc"))
        v_wmax, pe_wmax, v_wrow, pe_wrow, v_wscale, a_wh, v_wl = (sem(n) for n in (
            "v_wmax", "pe_wmax", "v_wrow", "pe_wrow", "v_wscale", "a_wh", "v_wl"))
        s_yk, s_last = [sem(f"s_yk{g}") for g in range(G - 1)], [sem(f"s_last{k}") for k in range(K)]
        a_first, c_ve, c_std, c_rstd, c_shift, a_last, c_fin = (sem(n) for n in (
            "a_first", "c_ve", "c_std", "c_rstd", "c_shift", "a_last", "c_fin"))
        s_out = sem("s_out")

        def ge(eng, s, n):
            if not isinstance(n, int) or n > 0:
                eng.wait_ge(s, n)

        def wait_apart(eng, s, n):
            if not isinstance(n, int):
                eng.to_reg(n)
            eng.wait_ge(s_const, 2)
            eng.wait_ge(s, n)

        def steps_value(eng, h):
            eng.wait_ge(v_tab, h + 1)
            return eng.value_load(steps_of[h][0:1, 0:1], min_val=TH * K // SLOTS - 3, max_val=MAX_BLOCKS // SLOTS - 3)

        def rows_loader(eng, name, n, used=None):
            regs = [eng.alloc_register(f"{name}{i}") for i in range(n)]

            def load(table, at, top):
                eng.load(regs, table[0:1, bass.ds(at, n)])
                return [eng.snap(regs[i], min_val=0, max_val=top) for i in used or range(n)]
            return load

        def stages(t=6, left=-1):
            return [n <= t and n > left for n in range(7)]

        def zero_tails(eng, load_four, h):
            eng.wait_ge(v_tab, h + 1)
            with eng.Fori(0, E // 4) as e:
                for r in load_four(tail_of[h], e * 4, E * REGION - P):
                    eng.dma_start(xs[h][bass.ds(r, P), :], zeros[:]).then_inc(s_tail[h], 16)

        block = ctx.enter_context(nc.Block())

        @block.sync
        def _(sp):
            sp.dma_start(x_sb[:, 0:GT, :], x_rows[:, 0:GT, :]).then_inc(s_x, 16)
            sp.dma_start(wi_raw[:], Wi).then_inc(s_wmix, 16)
            sp.dma_start(wr_raw[:], Wr).then_inc(s_wmix, 16)
            sp.dma_start(gate_raw[:], gate_w).then_inc(s_wmix, 16)
            with nc.allow_non_contiguous_dma(reason="one bias per channel"):
                sp.dma_start(bias_i[:], bi.rearrange("(p a) -> p a", a=1)).then_inc(s_small, 16)
                sp.dma_start(bias_r[:], br.rearrange("(p a) -> p a", a=1)).then_inc(s_small, 16)
                sp.dma_start(decay[:, 0:1], cap.rearrange("(a b) -> a b", a=1).to_broadcast([P, 1])).then_inc(s_small, 16)
                sp.dma_start(ebias[:], e_bias.rearrange("(a b) -> a b", a=1).to_broadcast([P, E])).then_inc(s_small, 16)
            for g in range(1, G):
                sp.wait_ge(s_x, 16 * g)
                sp.dma_start(x_sb[:, g * GT:(g + 1) * GT, :], x_rows[:, g * GT:(g + 1) * GT, :]).then_inc(s_x, 16)
            sp.wait_ge(s_const, 2)
            for h in range(HALVES):
                sp.dma_start(xs[h][E * REGION:E * REGION + SLOTS * P, :].rearrange("(n p) c -> p n c", p=P),
                             zeros[:].unsqueeze(1).to_broadcast([P, SLOTS, C])).then_inc(s_fill[h], 16)
                sp.dma_start(ys[h].rearrange("(n p) c -> p n c", p=P)[:, TH * K:, :],
                             zeros[:].unsqueeze(1).to_broadcast([P, MAX_BLOCKS - TH * K, C])).then_inc(s_fill[h], 16)
            four = rows_loader(sp, "row", SLOTS)

            def blocks(h, most_before):
                sp.wait_ge(s_fill[h], 32)
                sp.wait_ge(s_tail[h], 16 * E)
                sp.wait_ge(s_scat[h], 16 * TH * K)
                most = steps_value(sp, h)
                top = (E + 1) * REGION - P

                def load(r, u):
                    sp.dma_start(xb[:, u, :], xs[h][bass.ds(r, P), :]).then_inc(s_xb[h][u], 16)

                def step(q):
                    rows = four(row_of[h], q * SLOTS + SLOTS, top)
                    for p in range(2):
                        sp.wait_ge(b_xT[h], q * 2 + p + 1)
                        for u in (2 * p, 2 * p + 1):
                            load(rows[u], u)

                rows = four(row_of[h], 0, top)
                for u in range(SLOTS):
                    if h and u % 2 == 0:
                        wait_apart(sp, b_xT[h - 1], most_before * 2 + 5 + u // 2)
                    load(rows[u], u)
                with sp.Fori(0, most + 2) as q:
                    step(q)
                return most

            zero_tails(sp, four, 0)
            most_before = None
            for h in range(HALVES):
                most_before = blocks(h, most_before)
            for h in range(HALVES):
                for g in range(h * GH, h * GH + GH):
                    sp.wait_ge(c_fin, g + 1)
                    sp.dma_start(out_rows[:, g * GT:(g + 1) * GT, :], x_sb[:, g * GT:(g + 1) * GT, :]).then_inc(s_out, 16)
            sp.wait_ge(s_out, 16 * G)

        @block.gpsimd
        def _(pool):
            pool.memset(zeros[:], 0.0).then_inc(s_const, 1)
            pool.memset(ident[:], 0.0).then_inc(s_z0, 1)
            pool.memset(before[:], 1.0).then_inc(s_z0, 1)
            pool.memset(ones[:], 1.0)
            pool.memset(eps_c[:], EPS)
            pool.memset(ones_e[:], 1.0)
            pool.memset(seen[:], 0.0)
            pool.memset(ones_row[:], 1.0)
            pool.memset(wmax[:], 0.0)
            pool.iota(iota_e[:], pattern=[[1, E]], base=0, channel_multiplier=0, allow_small_or_imprecise_dtypes=True)
            pool.iota(region_e[:], pattern=[[REGION, E]], base=0, channel_multiplier=0, allow_small_or_imprecise_dtypes=True)
            pool.iota(iota_p[:], pattern=[[0, 1]], base=0, channel_multiplier=1, allow_small_or_imprecise_dtypes=True)
            pool.wait_ge(s_z0, 2)
            pool.affine_select(out=ident[:], in_=ident[:], compare_op=ALU.not_equal, fill=1.0, base=0,
                               pattern=[[-1, P]], channel_multiplier=1)
            pool.affine_select(out=before[:], in_=before[:], compare_op=ALU.is_ge, fill=0.0, base=-1,
                               pattern=[[1, P]], channel_multiplier=-1).then_inc(s_const, 1)
            for h in range(HALVES):
                for g in range(h * GH, h * GH + GH):
                    pool.wait_ge(v_row, g + 1)
                    pool.wait_ge(a_x2c, g + 1)
                    for j in range(GT):
                        for k in range(K):
                            pool.indirect_dma_start(
                                out=xs[h], out_offset=bass.IndirectOffsetOnAxis(
                                    ap=row_xs[:, (g * GT + j) * K + k:(g * GT + j) * K + k + 1], axis=0),
                                in_=xn2_all[:, g * GT + j, :],
                                in_offset=None).then_inc(s_scat[h], 16)
                if h:
                    zero_tails(pool, rows_loader(pool, "tail", 4), h)
            for h in range(HALVES):
                steps = steps_value(pool, h)
                for p in range(2):
                    wait_apart(pool, s_ys[h][p], steps * 16 + 48)
                pool.wait_ge(v_wl, 4)
                for g in range(h * GH, h * GH + GH):
                    pool.wait_ge(v_pack, g + 1)
                    for k in range(K):
                        for j in range(GT):
                            pool.indirect_dma_start(
                                out=yk[h][:, g * GT + j - h * TH, k, :], out_offset=None, in_=ys[h],
                                in_offset=bass.IndirectOffsetOnAxis(ap=row_ys[:, (g * GT + j) * K + k:(g * GT + j) * K + k + 1], axis=0),
                            ).then_inc(s_last[k] if g == G - 1 else s_yk[g], 16)

        @block.scalar
        def _(act):
            def norm(out, source, rstd, shift):
                for j in range(GT):
                    ins = act.activation(out[:, j, :], source(j), ACT.Identity, bias=shift[:, j:j + 1], scale=rstd[:, j:j + 1])
                return ins

            def norm_first(g):
                act.wait_ge(v_shift1, g + 1)
                ge(act, pe_xnT, g)
                norm(xn, lambda j: x_sb[:, bass.ds(g * GT + j, 1), :].rearrange("p a c -> p (a c)"),
                     rstd1, shift1).then_inc(a_xn, 1)

            def copy_first(g):
                act.wait_ge(pe_xnT, g + 1)
                ge(act, v_gated, g)
                ge(act, pe_z, g)
                act.copy(xnT[:], ps_xnT[:]).then_inc(a_xnT, 1)

            def gates(g):
                act.wait_ge(pe_zi, g + 1)
                act.activation(ti[:], ps_zi[:], ACT.Tanh, bias=bias_i[:], scale=0.5)
                act.wait_ge(pe_z, g + 1)
                act.activation(tr[:], ps_zr[:], ACT.Tanh, bias=bias_r[:], scale=0.5).then_inc(a_t, 1)

            def retained(g):
                act.wait_ge(a_t, g + 1)
                ge(act, v_scan, g)
                act.activation(at[:], tr[:], ACT.Exp, bias=decay[:, 5:6], scale=decay[:, 5:6]).then_inc(a_at, 1)
                act.wait_ge(a_at, g + 1)
                act.activation(at2[:], at[:], ACT.Square).then_inc(a_at2, 1)

            def std_first(g):
                act.wait_ge(v_var1, g + 1)
                act.activation(std1[:], mv1[:, :, 1], ACT.Sqrt, bias=eps_c[:]).then_inc(a_std1, 1)

            def root(g):
                act.wait_ge(a_at2, g + 1)
                act.activation(bq[:], at2[:], ACT.Sqrt, bias=decay[:, 4:5], scale=-0.25).then_inc(a_gate, 1)

            def std_mixed(g):
                act.wait_ge(v_varh, g + 1)
                act.activation(stdh[:], mvh[:, :, 1], ACT.Sqrt, bias=eps_c[:]).then_inc(a_stdh, 1)

            def std_second(g):
                act.wait_ge(v_var2, g + 1)
                act.activation(std2[:], mv2[:, :, 1], ACT.Sqrt, bias=eps_c[:]).then_inc(a_std2, 1)

            def norm_mixed(g):
                act.wait_ge(v_shifth, g + 1)
                ge(act, v_x1, g)
                norm(hn, lambda j: ps_h[:, j * P:(j + 1) * P], rstdh, shifth).then_inc(a_hn, 1)

            def norm_second(g):
                act.wait_ge(v_shift2, g + 1)
                ge(act, pe_x2T, g)
                ge(act, a_x2c, g)
                norm(xn2, lambda j: x_sb[:, bass.ds(g * GT + j, 1), :].rearrange("p a c -> p (a c)"),
                     rstd2, shift2).then_inc(a_xn2, 1)

            def copy_second(g):
                act.wait_ge(pe_x2T, g + 1)
                ge(act, pe_logit, g)
                act.copy(xn2T[:], ps_x2T[:]).then_inc(a_x2T, 1)

            def keep_second(g):
                act.wait_ge(a_xn2, g + 1)
                act.copy(xn2_all[:, bass.ds(g * GT, GT), :], xn2[:]).then_inc(a_x2c, 1)

            def scores(g):
                act.wait_ge(pe_logit, g + 1)
                act.activation(th_all[:, bass.ds(g * GT, GT), :].rearrange("p j e -> p (j e)"), ps_logit[:, 0:GT * E],
                               ACT.Tanh, scale=0.5).then_inc(a_th, 1)

            def step(s, mix, nxt, old, sec, rt):
                if mix:
                    gates(s)
                if rt:
                    scores(s - 3)
                if mix:
                    retained(s)
                if nxt:
                    std_first(s + 1)
                if mix:
                    root(s)
                if old:
                    std_mixed(s - 1)
                if sec:
                    std_second(s - 2)
                if nxt:
                    norm_first(s + 1)
                if old:
                    norm_mixed(s - 1)
                if sec:
                    norm_second(s - 2)
                if nxt:
                    copy_first(s + 1)
                if sec:
                    copy_second(s - 2)
                    keep_second(s - 2)

            act.wait_ge(s_const, 2)
            std_first(0)
            norm_first(0)
            copy_first(0)
            act.wait_ge(s_small, 64)
            act.wait_ge(s_wmix, 48)
            act.dma_start(w13_raw[:, :, 0, :], w1.rearrange("e h i -> h e i")).then_inc(s_wexp[0], 16)
            act.dma_start(w13_raw[:, :, 1, :], w3.rearrange("e h i -> h e i")).then_inc(s_wexp[1], 16)
            act.dma_start(w2_raw, w2.rearrange("e i h -> i e h")).then_inc(s_wexp[2], 16)
            act.activation(decay[:, 1:2], decay[:, 0:1], ACT.Abs).then_inc(l_act, 1)
            act.wait_ge(l_act, 1)
            act.activation(decay[:, 2:3], decay[:, 1:2], ACT.Exp, scale=-1.0).then_inc(l_act, 1)
            act.wait_ge(l_act, 2)
            act.activation(decay[:, 3:4], decay[:, 2:3], ACT.Ln, bias=1.0).then_inc(s_decay, 1)
            act.mul(bias_i[:], bias_i[:], 0.5)
            act.mul(bias_r[:], bias_r[:], 0.5).then_inc(s_bias, 1)
            act.wait_ge(s_bias, 1)
            act.wait_ge(s_decay, 2)
            for s in range(4):
                step(s, True, True, s >= 1, s >= 2, s >= 3)
            with act.Fori(4, G - 1) as s:
                step(s, True, True, True, True, True)
            act.wait_ge(v_wscale, 1)
            for s in range(G - 1, G + 3):
                e = slice((s - G + 1) * E // 4, (s - G + 2) * E // 4)
                act.activation(w13_h[:, e, :, :], w13_raw[:, e, :, :], ACT.Identity, scale=wscale[:, 0:1])
                act.activation(w2_h[:, e, :], w2_raw[:, e, :], ACT.Identity, scale=wscale[0:I, 1:2]).then_inc(a_wh, 1)
                step(s, s < G, False, s <= G, s <= G + 1, True)

            most = [steps_value(act, h) for h in range(HALVES)]
            act.preload_act_table(ACT.Tanh)

            def slot(h, t, p, on):
                o = 1 - p
                if on[4]:
                    act.wait_ge(b_aT[h], t - 3)
                    act.copy(aT[:, p, :, :, :].rearrange("i b f t -> i (b f t)"),
                             ps_aT[p][0:I, :].bitcast(F16)[:, 0:4 * P]).then_inc(b_aTc[h], 1)
                if on[0]:
                    act.wait_ge(b_xT[h], t + 1)
                    act.copy(xbT_h[:, p, :, :].rearrange("c b t -> c (b t)"), ps_xbT[p][:, 0:2 * P]).then_inc(b_xh[h], 1)
                if on[5]:
                    act.wait_ge(b_yc[h], t - 4)
                    act.dma_start(ys[h][bass.ds((t - 5) * (2 * P), 2 * P), :].rearrange("(b p) c -> p b c", p=P),
                                  yb[:, o, :, :]).then_inc(s_ys[h][o], 16)
                if on[1]:
                    act.wait_ge(b_gu[h], t)
                    act.activation(act_t[:, o, :, :], ps_gu[o][:, 0:4 * I].rearrange(
                        "t (b w i) -> t b w i", b=2, w=2)[:, :, 0, :], ACT.Tanh, scale=wscale[:, 2:3]).then_inc(b_tanh[h], 1)
                if on[4]:
                    act.wait_ge(b_y[h], t - 3)
                    act.copy(y2[:, p, :, :], ps_y[p][:].rearrange("t (b f c) -> t b f c", b=2, f=2)[:, :, 1, :]).then_inc(
                        b_y2[h], 1)

            for h in range(HALVES):
                for t in range(6):
                    if h:
                        if t < 5:
                            slot(0, most[0] * 2 + 6 + t, t % 2, stages(left=t))
                        if t == 4:
                            wait_apart(act, b_y[0], most[0] * 2 + 6)
                    slot(h, t, t % 2, stages(t))
                with act.Fori(1, most[h] + 1) as q:
                    for p in range(2):
                        slot(h, q * 2 + 4 + p, p, stages())
            for t in range(5):
                slot(1, most[1] * 2 + 6 + t, t % 2, stages(left=t))

            def first_choice(g):
                h, b = int(g >= GH), g % 3
                act.wait_ge(v_wt, g + 1)
                if g >= 3:
                    act.wait_ge(c_fin, g - 2)
                if g == G - 1:
                    act.wait_ge(s_last[0], 16 * GT)
                else:
                    act.wait_ge(s_yk[g], 16 * GT * K)
                for j in range(GT):
                    t = g * GT + j
                    ins = act.activation(mix[b][:, j, :], yk[h][:, t - h * TH, 0, :], ACT.Identity, scale=wt_all[:, t, 0:1])
                ins.then_inc(a_first, 1)

            def norm_last(g):
                b = g % 3
                act.wait_ge(c_shift, g + 1)
                for j in range(GT):
                    ins = act.activation(mix[b][:, j, :], mix[b][:, j, :], ACT.Identity,
                                         bias=shift3[:, g % 2, j:j + 1], scale=rstd3[:, g % 2, j:j + 1])
                ins.then_inc(a_last, 1)

            for g in range(G):
                first_choice(g)
                if g:
                    norm_last(g - 1)
                act.wait_ge(c_ve, g + 1)
                act.activation(std3[:, g % 2, :], mv3[:, g % 2, :, 1], ACT.Sqrt, bias=eps_c[:]).then_inc(c_std, 1)
            norm_last(G - 1)

        @block.vector
        def _(dve):
            def bn(source, st):
                for j in range(GT):
                    ins = dve.bn_stats(st[:, j, :], source(j))
                return ins

            def aggregate(st, mv):
                for j in range(GT):
                    ins = dve.bn_aggr(mv[:, j, :], st[:, j, :])
                return ins

            def x_tile(g):
                return lambda j: x_sb[:, bass.ds(g * GT + j, 1), :].rearrange("p a c -> p (a c)")

            def stats_first(g):
                wait_apart(dve, s_x, 16 * (g + 1))
                bn(x_tile(g), st1).then_inc(v_st1, 1)

            def var_first(g):
                wait_apart(dve, v_st1, g + 1)
                ge(dve, v_shift1, g)
                aggregate(st1, mv1).then_inc(v_var1, 1)

            def rstd(g, a_std, r, std, v_rstd):
                dve.wait_ge(a_std, g + 1)
                dve.reciprocal(r[:], std[:]).then_inc(v_rstd, 1)

            def shift(g, v_rstd, r, mv, out, v_shift):
                dve.wait_ge(v_rstd, g + 1)
                dve.scalar_tensor_tensor(out=out[:], in0=mv[:, :, 0], scalar=-1.0, in1=r[:],
                                         op0=ALU.mult, op1=ALU.mult).then_inc(v_shift, 1)

            def recur(g):
                dve.wait_ge(a_gate, g + 1)
                dve.scalar_tensor_tensor(out=gated[:], in0=ti[:], scalar=1.0, in1=xnT[:],
                                         op0=ALU.add, op1=ALU.mult).then_inc(v_gated, 1)
                dve.wait_ge(v_gated, g + 1)
                dve.tensor_tensor(gx[:], bq[:], gated[:], ALU.mult).then_inc(v_gx, 1)

            def scan(g):
                dve.wait_ge(v_gx, g + 1)
                ge(dve, pe_h, g)
                for t in range(0, GC, SEQ):
                    ins = dve.tensor_tensor_scan(hT[:, t:t + SEQ], at[:, t:t + SEQ], gx[:, t:t + SEQ], 0.0,
                                                 ALU.mult, ALU.add)
                ins.then_inc(v_scan, 1)

            def add_mixed(g):
                dve.wait_ge(a_hn, g + 1)
                dve.tensor_tensor(x_sb[:, bass.ds(g * GT, GT), :], x_sb[:, bass.ds(g * GT, GT), :], hn[:],
                                  ALU.add).then_inc(v_x1, 1)

            def choose(g):
                dve.wait_ge(a_th, g + 1)
                dve.scalar_tensor_tensor(out=biased[:], in0=th_all[:, bass.ds(g * GT, GT), :], scalar=0.5,
                                         in1=ebias_half[:].unsqueeze(1).to_broadcast([P, GT, E]),
                                         op0=ALU.mult, op1=ALU.add).then_inc(v_biased, 1)

            def best(g):
                wait_apart(dve, v_biased, g + 1)
                for j in range(GT):
                    ins = dve.max(top[:, j, :], biased[:, j, :])
                ins.then_inc(v_top, 1)

            def best_experts(g):
                wait_apart(dve, v_top, g + 1)
                for j in range(GT):
                    ins = dve.max_index(top_i[:, j, :], top[:, j, :], biased[:, j, :])
                ins.then_inc(v_top_i, 1)

            def one_hot(g):
                dve.wait_ge(v_top_f, g + 1)
                dve.tensor_tensor(hot_all[:, bass.ds(g * GT, GT), :, :],
                                  iota_e[:].unsqueeze(1).unsqueeze(1).to_broadcast([P, GT, K, E]),
                                  top_f[:].unsqueeze(3).to_broadcast([P, GT, K, E]), ALU.is_equal).then_inc(v_hot, 1)

            def masks(g):
                wait_apart(dve, v_hot, g + 1)
                ge(dve, pe_pos, g)
                with nc.allow_low_precision(reason="a mask of zeros and ones"):
                    dve.tensor_reduce(mask[:], hot_all[:, bass.ds(g * GT, GT), :, :].rearrange("p j k e -> p j e k"),
                                      AX_X, ALU.add).then_inc(v_mask, 1)

            def count(g, reset=0):
                dve.wait_ge(v_mask, g + 1)
                dve.tensor_reduce(add4[:], mask[:].rearrange("p j e -> p e j"), AX_X, ALU.add).then_inc(v_add4, 1)
                dve.wait_ge(pe_pos, g + 1)
                dve.tensor_tensor(pos[:], ps_pos[:, 0:GT * E].rearrange("p (j e) -> p j e", j=GT),
                                  region_e[:].unsqueeze(1).to_broadcast([P, GT, E]), ALU.add).then_inc(v_pos, 1)
                dve.wait_ge(v_add4, g + 1)
                with nc.allow_low_precision(reason="counts of at most 16"):
                    dve.tensor_tensor(seen[:], seen[:], add4[:], ALU.add).then_inc(v_seen, 1)

            def rows(g):
                dve.wait_ge(v_pos, g + 1)
                dve.tensor_tensor(picked[:], hot_all[:, bass.ds(g * GT, GT), :, :],
                                  pos[:].unsqueeze(2).to_broadcast([P, GT, K, E]), ALU.mult).then_inc(v_picked, 1)
                wait_apart(dve, v_picked, g + 1)
                group = row_f[:, bass.ds(g * GT, GT), :]
                dve.tensor_reduce(group, picked[:], AX_X, ALU.add).then_inc(v_rowf, 1)
                dve.wait_ge(v_rowf, g + 1)
                dve.tensor_copy(row_xs[:, bass.ds(g * GT * K, GT * K)].rearrange("p (j k) -> p j k", j=GT),
                                group).then_inc(v_row, 1)

            def step(s, mix, nxt, old, sec, rt, between=None, before=None):
                if sec:
                    add_mixed(s - 2)
                if old:
                    wait_apart(dve, pe_h, s)
                    bn(lambda j: ps_h[:, j * P:(j + 1) * P], sth).then_inc(v_sth, 1)
                if sec:
                    wait_apart(dve, v_x1, s - 1)
                    bn(x_tile(s - 2), st2).then_inc(v_st2, 1)
                if nxt:
                    stats_first(s + 1)
                if sec:
                    wait_apart(dve, v_st2, s - 1)
                    aggregate(st2, mv2).then_inc(v_var2, 1)
                if old:
                    wait_apart(dve, v_sth, s)
                    aggregate(sth, mvh).then_inc(v_varh, 1)
                if before:
                    before()
                if rt:
                    choose(s - 3)
                if nxt:
                    var_first(s + 1)
                if rt:
                    best(s - 3)
                    best_experts(s - 3)
                    dve.wait_ge(v_top_i, s - 2)
                    dve.tensor_copy(top_f[:], top_i[:, :, 0:K]).then_inc(v_top_f, 1)
                if rt:
                    one_hot(s - 3)
                    masks(s - 3)
                if nxt:
                    rstd(s + 1, a_std1, rstd1, std1, v_rstd1)
                if old:
                    rstd(s - 1, a_stdh, rstdh, stdh, v_rstdh)
                if nxt:
                    shift(s + 1, v_rstd1, rstd1, mv1, shift1, v_shift1)
                if sec:
                    rstd(s - 2, a_std2, rstd2, std2, v_rstd2)
                if old:
                    shift(s - 1, v_rstdh, rstdh, mvh, shifth, v_shifth)
                if sec:
                    shift(s - 2, v_rstd2, rstd2, mv2, shift2, v_shift2)
                if between:
                    between()
                if rt:
                    count(s - 3)
                    rows(s - 3)
                if mix:
                    recur(s)
                if mix:
                    scan(s)

            def tables(h):
                n = [h * DVE_TABLES + 1]

                def count(ins):
                    n[0] += 1
                    ins.then_inc(l_tab, 1)

                def link(ins):
                    count(ins)
                    dve.wait_ge(l_tab, n[0])

                dve.wait_ge(pe_cnt, h + 1)
                count(dve.tensor_copy(cnt[:], ps_pos[:, 128:128 + E]))
                if h == 0:
                    dve.wait_ge(v_seen, GH)
                    dve.memset(seen[:], 0.0).then_inc(v_seen, 1)
                link(dve.tensor_scalar(cnt_up[:], ps_pos[:, 128:128 + E], float(P - 1), None, ALU.add))
                link(dve.tensor_scalar(nblk_i[:], cnt_up[:], 7, None, ALU.logical_shift_right))
                link(dve.tensor_copy(nblk[:], nblk_i[:]))
                link(dve.tensor_tensor_scan(cum[:], ones_e[:], nblk[:], 0.0, ALU.mult, ALU.add))
                count(dve.tensor_scalar(steps_u[:, 0:1], cum[0:1, E - 1:E], -1.0 - 2.0 * SLOTS, None, ALU.add))
                link(dve.tensor_scalar(past[:], cum[:], iota_p[:], None, ALU.is_le))
                count(dve.tensor_tensor(past_n[:], past[:], nblk[:], ALU.mult))
                count(dve.tensor_scalar(steps_of[h][:], steps_u[:, 0:1], SLOTS.bit_length() - 1, None, ALU.logical_shift_right))
                link(dve.tensor_reduce(tcol[:, 0:1], past[:], AX_X, ALU.add))
                count(dve.tensor_reduce(tcol[:, 1:2], past_n[:], AX_X, ALU.add))
                count(dve.tensor_scalar(tcol[:, 2:3], tcol[:, 0:1], float(E - 1), None, ALU.min))
                link(dve.tensor_scalar(tcol[:, 4:5], tcol[:, 0:1], float(REGION), None, ALU.mult))
                link(dve.tensor_tensor(tcol[:, 3:4], iota_p[:], tcol[:, 1:2], ALU.subtract))
                count(dve.scalar_tensor_tensor(out=tcol[:, 5:6], in0=tcol[:, 3:4], scalar=float(P), in1=tcol[:, 4:5],
                                               op0=ALU.mult, op1=ALU.add))
                dve.tensor_tensor(past_n[:], cnt[:], region_e[:], ALU.add).then_inc(v_tcol, 1)
                dve.wait_ge(v_tcol, h + 1)
                dve.tensor_copy(tail_of[h][:], past_n[0:1, :])
                dve.wait_ge(pe_tab, h + 1)
                link(dve.tensor_copy(expert_of[h][:], ps_setup[0:1, 0:P]))
                dve.tensor_copy(row_of[h][:], ps_setup[0:1, P:2 * P]).then_inc(v_tab, 1)
                link(dve.tensor_tensor(past[:], cum[:], nblk[:], ALU.subtract))
                assert n[0] == (h + 1) * DVE_TABLES + 1
                dve.scalar_tensor_tensor(out=pack[h][:], in0=past[:], scalar=float(P), in1=region_e[:],
                                         op0=ALU.mult, op1=ALU.subtract).then_inc(v_shift, 1)

            def result_rows(groups):
                for g in groups:
                    h, n = g // GH, g * 2
                    dve.wait_ge(v_shift, h + 1)
                    if n:
                        dve.wait_ge(l_pack, n)
                        dve.wait_ge(v_pack, g)
                    dve.tensor_tensor(shifts[:], hot_all[:, g * GT:(g + 1) * GT, :, :],
                                      pack[h][:].unsqueeze(1).unsqueeze(1).to_broadcast([P, GT, K, E]),
                                      ALU.mult).then_inc(l_pack, 1)
                    dve.wait_ge(l_pack, n + 1)
                    dve.tensor_reduce(shift_f[:], shifts[:], AX_X, ALU.add).then_inc(l_pack, 1)
                    dve.wait_ge(l_pack, n + 2)
                    dve.tensor_tensor(row_ys[:, g * GT * K:(g + 1) * GT * K].rearrange("p (j k) -> p j k", j=GT),
                                      row_f[:, g * GT:(g + 1) * GT, :], shift_f[:], ALU.add).then_inc(v_pack, 1)

            def weights_max(part):
                dve.wait_ge(s_wexp[part], 16)
                raw = w13_raw[:, :, part, :] if part < 2 else w2_raw
                dve.tensor_reduce(wmax[0:raw.shape[0], part:part + 1], raw, AX_XY, ALU.max,
                                  apply_absolute_value=True).then_inc(v_wmax, 1)

            def weights_scale():
                n = [0]

                def link(ins):
                    n[0] += 1
                    ins.then_inc(v_wrow, 1)
                    dve.wait_ge(v_wrow, n[0])

                dve.wait_ge(pe_wmax, 1)
                link(dve.tensor_reduce(wtop3[:], ps_setup[0:1, 0:3 * P].rearrange("a (w p) -> a w p", w=3), AX_X, ALU.max))
                link(dve.tensor_scalar(wtop[:], wtop3[:, 1:3], 2.0 ** -60, None, ALU.max))
                link(dve.tensor_tensor(wtop[:, 0:1], wtop[:, 0:1], wtop3[:, 0:1], ALU.max))
                link(dve.tensor_scalar(wpow[:].bitcast(U32), wtop[:].bitcast(U32), 0x7F800000, None, ALU.bitwise_and))
                link(dve.tensor_scalar(wrow[:, 4:6], wpow[:], 2.0, None, ALU.mult))
                link(dve.reciprocal(wrow[:, 0:2], wrow[:, 4:6]))
                link(dve.tensor_copy(wrow[:, 2:3], wpow[:, 0:1]))
                link(dve.tensor_tensor(wrow[:, 6:7], wrow[:, 4:5], wrow[:, 4:5], ALU.mult))
                link(dve.tensor_tensor(wrow[:, 3:4], wrow[:, 6:7], wpow[:, 1:2], ALU.mult))

            def weights_rest(quarter):
                dve.wait_ge(a_wh, quarter + 1)
                e = slice(quarter * E // 4, (quarter + 1) * E // 4)
                dve.scalar_tensor_tensor(out=w13_l[:, e, :, :], in0=w13_raw[:, e, :, :], scalar=wscale[:, 0:1],
                                         in1=w13_h[:, e, :, :], op0=ALU.mult, op1=ALU.subtract)
                dve.scalar_tensor_tensor(out=w2_l[:, e, :], in0=w2_raw[:, e, :], scalar=wscale[0:I, 1:2],
                                         in1=w2_h[:, e, :], op0=ALU.mult, op1=ALU.subtract).then_inc(v_wl, 1)

            stats_first(0)
            var_first(0)
            rstd(0, a_std1, rstd1, std1, v_rstd1)
            shift(0, v_rstd1, rstd1, mv1, shift1, v_shift1)
            dve.wait_ge(s_setT, 1)
            dve.tensor_copy(wiT[:], ps_setup[:, 0:P])
            dve.tensor_copy(wrT[:], ps_setup[:, P:2 * P])
            dve.tensor_copy(gateT[:], ps_setup[:, 2 * P:2 * P + E]).then_inc(s_wT, 1)
            dve.wait_ge(s_const, 2)
            dve.tensor_copy(ident_h[:], ident[:]).then_inc(s_wT, 1)
            dve.wait_ge(s_small, 64)
            dve.tensor_scalar(ebias_half[:], ebias[:], 0.5, None, ALU.add).then_inc(v_ebias, 1)
            dve.wait_ge(v_ebias, 1)
            dve.memset(decay[:, 4:5], 0.25)
            dve.wait_ge(s_decay, 1)
            dve.scalar_tensor_tensor(out=decay[:, 5:6], in0=decay[:, 0:1], scalar=0.0, in1=decay[:, 3:4],
                                     op0=ALU.max, op1=ALU.add).then_inc(l_tab, 1)
            dve.wait_ge(l_tab, 1)
            dve.tensor_scalar(decay[:, 5:6], decay[:, 5:6], -4.0, None, ALU.mult).then_inc(s_decay, 1)
            for s in range(4):
                step(s, True, True, s >= 1, s >= 2, s >= 3,
                     between=[None, lambda: weights_max(0), lambda: (weights_max(1), weights_max(2)), weights_scale][s])
            with dve.Fori(4, GH + 3) as s:
                step(s, True, True, True, True, True)
            dve.wait_ge(pe_wrow, 1)
            dve.tensor_copy(wscale[:, 0:4], ps_setup[:, 0:4]).then_inc(v_wscale, 1)
            for s in range(GH + 3, G + 3):
                step(s, s < G, s + 1 < G, s <= G, s <= G + 1, True, between=lambda: weights_rest(s - G + 1),
                     before=[lambda: tables(0), None, lambda: result_rows((0, 1)), lambda: result_rows((2, 3))][s - G + 1])
            tables(1)

            most = [steps_value(dve, h) for h in range(HALVES)]

            def slot(h, t, q, p, on):
                gu = ps_gu[p][:, 0:4 * I].rearrange("t (b w i) -> t b w i", b=2, w=2)
                if on[2]:
                    dve.wait_ge(b_tanh[h], t - 1)
                    dve.scalar_tensor_tensor(out=silu2[:, p, :, :], in0=act_t[:, p, :, :], scalar=1.0,
                                             in1=gu[:, :, 0, :], op0=ALU.add, op1=ALU.mult).then_inc(b_silu[h], 1)
                if on[2]:
                    dve.wait_ge(b_silu[h], t - 1)
                    if on[4]:
                        dve.wait_ge(b_al[h], t - 3)
                    dve.tensor_tensor(act_a[:, p, :, :], silu2[:, p, :, :], gu[:, :, 1, :], ALU.mult).then_inc(b_act[h], 1)
                if on[0]:
                    dve.wait_ge(b_xh[h], t + 1)
                    dve.tensor_tensor(xbT_l[:, p, :, :].rearrange("c b t -> c (b t)"), ps_xbT[p][:, 0:2 * P],
                                      xbT_h[:, p, :, :].rearrange("c b t -> c (b t)"), ALU.subtract).then_inc(b_xl[h], 1)
                if on[2]:
                    dve.wait_ge(b_act[h], t - 1)
                    if not on[0]:
                        dve.wait_ge(b_aT[h], t - 3)
                    dve.tensor_copy(act_h[:, p, :, :], act_a[:, p, :, :]).then_inc(b_ah[h], 1)
                    dve.wait_ge(b_ah[h], t - 1)
                    dve.tensor_tensor(act_l[:, p, :, :], act_a[:, p, :, :], act_h[:, p, :, :], ALU.subtract).then_inc(b_al[h], 1)
                if on[4]:
                    dve.wait_ge(b_y2[h], t - 3)
                    if on[6]:
                        dve.wait_ge(s_ys[h][p], q * 16)
                    dve.tensor_tensor(yb[:, p, :, :], ps_y[p][:].rearrange("t (b f c) -> t b f c", b=2, f=2)[:, :, 0, :],
                                      y2[:, p, :, :], ALU.add).then_inc(b_yc[h], 1)

            for h in range(HALVES):
                for t in range(6):
                    if h:
                        if t < 4:
                            slot(0, most[0] * 2 + 6 + t, most[0] + 1 + t // 2, t % 2, stages(left=t))
                        if t == 2:
                            wait_apart(dve, b_al[0], most[0] * 2 + 6)
                        if t >= 4:
                            wait_apart(dve, s_ys[0][t - 4], most[0] * 16 + 48)
                    slot(h, t, t // 2 - 2, t % 2, stages(t))
                with dve.Fori(1, most[h] + 1) as q:
                    for p in range(2):
                        slot(h, q * 2 + 4 + p, q, p, stages())
            for t in range(4):
                slot(1, most[1] * 2 + 6 + t, most[1] + 1 + t // 2, t % 2, stages(left=t))
            result_rows(range(GH, G))

            def weigh(g, part):
                if g >= G:
                    return
                tiles = slice(g * GT, (g + 1) * GT)
                if part == 0:
                    if g:
                        dve.wait_ge(v_wt, g)
                    dve.tensor_tensor(picked[:], hot_all[:, tiles, :, :],
                                      th_all[:, tiles, :].unsqueeze(2).to_broadcast([P, GT, K, E]),
                                      ALU.mult).then_inc(v_chosen, 1)
                if part == 1:
                    dve.wait_ge(v_chosen, g + 1)
                    dve.tensor_reduce(wsel[:], picked[:], AX_X, ALU.add).then_inc(v_wsel, 1)
                if part == 2:
                    dve.wait_ge(v_wsel, g + 1)
                    dve.tensor_scalar(wscore[:], wsel[:], 0.5, 0.5, ALU.mult, ALU.add).then_inc(v_wscore, 1)
                if part == 3:
                    dve.wait_ge(v_wscore, g + 1)
                    dve.tensor_reduce(wsum[:], wscore[:], AX_X, ALU.add).then_inc(v_wsum, 1)
                if part == 4:
                    dve.wait_ge(v_wsum, g + 1)
                    dve.reciprocal(winv[:], wsum[:]).then_inc(v_winv, 1)
                if part == 5:
                    dve.wait_ge(v_winv, g + 1)
                    dve.scalar_tensor_tensor(out=wt_all[:, tiles, :], in0=wscore[:], scalar=wscale[:, 3:4],
                                             in1=winv[:].unsqueeze(2).to_broadcast([P, GT, K]),
                                             op0=ALU.mult, op1=ALU.mult).then_inc(v_wt, 1)

            def inverse(g):
                dve.wait_ge(c_std, g + 1)
                dve.reciprocal(rstd3[:, g % 2, :], std3[:, g % 2, :]).then_inc(c_rstd, 1)

            def shift_last(g):
                dve.wait_ge(c_rstd, g + 1)
                dve.scalar_tensor_tensor(out=shift3[:, g % 2, :], in0=mv3[:, g % 2, :, 0], scalar=-1.0,
                                         in1=rstd3[:, g % 2, :], op0=ALU.mult, op1=ALU.mult).then_inc(c_shift, 1)

            def add_last(g):
                dve.wait_ge(a_last, g + 1)
                dve.tensor_tensor(x_sb[:, g * GT:(g + 1) * GT, :], mix[g % 3][:], x_sb[:, g * GT:(g + 1) * GT, :],
                                  ALU.add).then_inc(c_fin, 1)

            def combine(g, h):
                b = g % 3
                dve.wait_ge(a_first, g + 1)
                for k in range(1, K):
                    if g == G - 1:
                        dve.wait_ge(s_last[k], 16 * GT)
                    if k > 1:
                        dve.wait_ge(l_mix, g * K + k - 1)
                    for j in range(GT):
                        t = g * GT + j
                        ins = dve.scalar_tensor_tensor(out=mix[b][:, j, :], in0=yk[h][:, t - h * TH, k, :],
                                                       scalar=wt_all[:, t, k:k + 1], in1=mix[b][:, j, :],
                                                       op0=ALU.mult, op1=ALU.add)
                    ins.then_inc(l_mix, 1)
                    weigh(g + 2, k - 1)
                    if k == 1 and g:
                        inverse(g - 1)
                    if k == 2 and g:
                        shift_last(g - 1)
                dve.wait_ge(l_mix, g * K + K - 1)
                bn(lambda j: mix[b][:, j, :], st3).then_inc(l_mix, 1)
                weigh(g + 2, 3)
                if g:
                    add_last(g - 1)
                weigh(g + 2, 4)
                dve.wait_ge(l_mix, g * K + K)
                aggregate(st3, mv3[:, g % 2, :, :]).then_inc(c_ve, 1)
                weigh(g + 2, 5)

            for g in range(2):
                for part in range(6):
                    weigh(g, part)
            for g in range(G):
                combine(g, int(g >= GH))
            inverse(G - 1)
            shift_last(G - 1)
            add_last(G - 1)

        @block.tensor
        def _(pe):
            pe.wait_ge(s_const, 2)
            pe.wait_ge(s_wmix, 48)
            pe.transpose(ps_setup[:, 0:P], wi_raw[:], ident[:])
            pe.transpose(ps_setup[:, P:2 * P], wr_raw[:], ident[:])
            pe.transpose(ps_setup[:, 2 * P:2 * P + E], gate_raw[:], ident[0:E, 0:E]).then_inc(s_setT, 1)

            def turn_first(g):
                pe.wait_ge(a_xn, g + 1)
                ge(pe, a_xnT, g)
                for j in range(GT):
                    ins = pe.transpose(ps_xnT[:, j * P:(j + 1) * P], xn[:, j, :], ident[:])
                ins.then_inc(pe_xnT, 1)

            def mixer(g):
                pe.wait_ge(a_xnT, g + 1)
                pe.matmul(ps_zi[:], wiT[:], xnT[:], start=True, stop=True).then_inc(pe_zi, 1)
                pe.matmul(ps_zr[:], wrT[:], xnT[:], start=True, stop=True).then_inc(pe_z, 1)

            def mixed(g):
                pe.wait_ge(v_scan, g + 1)
                ge(pe, a_hn, g)
                for j in range(GT):
                    ins = pe.transpose(ps_h[:, j * P:(j + 1) * P], hT[:, j * P:(j + 1) * P], ident[:])
                ins.then_inc(pe_h, 1)

            def turn_second(g):
                pe.wait_ge(a_xn2, g + 1)
                ge(pe, a_x2T, g)
                for j in range(GT):
                    ins = pe.transpose(ps_x2T[:, j * P:(j + 1) * P], xn2[:, j, :], ident[:])
                ins.then_inc(pe_x2T, 1)

            def router(g):
                pe.wait_ge(a_x2T, g + 1)
                ge(pe, a_th, g)
                for j in range(GT):
                    ins = pe.matmul(ps_logit[:, j * E:(j + 1) * E], xn2T[:, j * P:(j + 1) * P], gateT[:],
                                    start=True, stop=True)
                ins.then_inc(pe_logit, 1)

            def positions(g, reset):
                pe.wait_ge(v_mask, g + 1)
                ge(pe, v_seen, g + reset)
                for j in range(GT):
                    dst = ps_pos[:, j * E:(j + 1) * E]
                    pe.matmul(dst, ones[:], seen[:], start=True, stop=False)
                    for i in range(j):
                        pe.matmul(dst, ones[:], mask[:, i, :], start=False, stop=False)
                    ins = pe.matmul(dst, before[:], mask[:, j, :], start=False, stop=True)
                ins.then_inc(pe_pos, 1)

            def tables(h):
                pe.wait_ge(v_seen, (h + 1) * GH + h)
                pe.matmul(ps_pos[:, 128:128 + E], ones[:], seen[:], start=True, stop=True).then_inc(pe_cnt, 1)
                pe.wait_ge(v_tcol, h + 1)
                pe.transpose(ps_setup[0:1, 0:P], tcol[:, 2:3], ident[:])
                pe.transpose(ps_setup[0:1, P:2 * P], tcol[:, 5:6], ident[:]).then_inc(pe_tab, 1)

            def step(s, mix, nxt, sec, rt, reset=0):
                if rt:
                    positions(s - 3, reset)
                if nxt:
                    turn_first(s + 1)
                if sec:
                    turn_second(s - 2)
                if mix:
                    mixed(s)
                if nxt:
                    mixer(s + 1)
                if sec:
                    router(s - 2)

            turn_first(0)
            pe.wait_ge(s_wT, 2)
            mixer(0)
            for s in range(4):
                step(s, True, True, s >= 2, s >= 3)
                if s == 2:
                    pe.wait_ge(v_wmax, 3)
                    for part in range(3):
                        ins = pe.transpose(ps_setup[0:1, part * P:(part + 1) * P], wmax[:, part:part + 1], ident[:])
                    ins.then_inc(pe_wmax, 1)
            pe.wait_ge(v_wrow, 9)
            pe.matmul(ps_setup[:, 0:4], ones_row[:], wrow[:, 0:4], start=True, stop=True).then_inc(pe_wrow, 1)
            with pe.Fori(4, GH + 3) as s:
                step(s, True, True, True, True)
            tables(0)
            for s in range(GH + 3, G + 3):
                step(s, s < G, s + 1 < G, s < G + 2, True, 1)
            tables(1)

            pe.wait_ge(v_wl, 4)
            experts = rows_loader(pe, "expert", 10, (0, 1, 2, 3, 6, 7, 8, 9))
            most = [steps_value(pe, h) for h in range(HALVES)]

            def slot(h, t, q, p, on, e_gu, e_y):
                o = 1 - p
                if on[0]:
                    for b in range(2):
                        pe.wait_ge(s_xb[h][2 * p + b], q * 16 + 48)
                        ins = pe.transpose(ps_xbT[p][:, b * P:(b + 1) * P], xb[:, 2 * p + b, :], ident[:])
                    ins.then_inc(b_xT[h], 1)
                if on[1]:
                    pe.wait_ge(b_xl[h], t)
                    for b in range(2):
                        dst = ps_gu[o][:, b * 2 * I:(b + 1) * 2 * I]
                        w_h, w_l = (w13[:, bass.ds(e_gu[b], 1), f, :, :].rearrange("c a w i -> c (a w i)") for f in range(2))
                        pe.matmul(dst, xbT_h[:, o, b, :], w_h, start=True, stop=False)
                        pe.matmul(dst, xbT_h[:, o, b, :], w_l, start=False, stop=False)
                        ins = pe.matmul(dst, xbT_l[:, o, b, :], w_h, start=False, stop=True)
                    ins.then_inc(b_gu[h], 1)
                if on[4]:
                    pe.wait_ge(b_aTc[h], t - 3)
                    for b in range(2):
                        dst = ps_y[p][:, b * 2 * P:(b + 1) * 2 * P]
                        w_both = w2s[:, bass.ds(e_y[b], 1), :, :].rearrange("i a f c -> i (a f c)")
                        pe.matmul(dst, aT[:, p, b, 0, :], w_both, start=True, stop=False)
                        ins = pe.matmul(dst[:, 0:P], aT[:, p, b, 1, :], w_both[:, 0:C], start=False, stop=True)
                    ins.then_inc(b_y[h], 1)
                if on[3]:
                    pe.wait_ge(b_al[h], t - 2)
                    aT16 = ps_aT[o][0:I, :].bitcast(F16)
                    for b in range(2):
                        for f, part in enumerate((act_h, act_l)):
                            at16 = (2 * b + f) * P
                            ins = pe.transpose(aT16[:, at16:at16 + P], part[:, o, b, :], ident_h[:])
                    ins.then_inc(b_aT[h], 1)

            def step_experts(h, q):
                if isinstance(q, int) and q == -2:
                    return [None] * 6 + experts(expert_of[h], 0, E - 1)[0:2]
                if isinstance(q, int) and q == -1:
                    return [None] * 4 + experts(expert_of[h], 2, E - 1)[0:4]
                return experts(expert_of[h], q * SLOTS, E - 1)

            def half_step(h, t, q, p, e, on):
                slot(h, t + p, q, p, on, e[4 + 2 * p:6 + 2 * p], e[2 * p:2 * p + 2])

            for h in range(HALVES):
                for t in (0, 2, 4):
                    e = step_experts(h, t // 2 - 2)
                    if h and t < 4:
                        e_old = step_experts(0, most[0] + 1 + t // 2)
                    if h and t == 4:
                        wait_apart(pe, b_yc[0], most[0] * 2 + 6)
                    for p in range(2):
                        if h and t < 4:
                            half_step(0, most[0] * 2 + 6 + t, most[0] + 1 + t // 2, p, e_old, stages(left=t + p))
                        half_step(h, t, t // 2 - 2, p, e, stages(t + p))
                with pe.Fori(1, most[h] + 1) as q:
                    e = step_experts(h, q)
                    for p in range(2):
                        half_step(h, q * 2 + 4, q, p, e, stages())
            for t in (0, 2):
                e = step_experts(1, most[1] + 1 + t // 2)
                for p in range(2):
                    half_step(1, most[1] * 2 + 6 + t, most[1] + 1 + t // 2, p, e, stages(left=t + p))


_INS = ["L0_attn_x", "L0_attn_Wi", "L0_attn_bi", "L0_attn_Wr", "L0_attn_br", "L0_attn_cap_lambda",
        "L0_ffn_gate_w", "L0_ffn_w1", "L0_ffn_w3", "L0_ffn_w2", "L0_ffn_e_bias"]


def kernel(**inputs):
    import numpy as _np
    import concourse.bacc as _bacc
    from concourse import mybir as _mybir
    from concourse.bass_utils import run_bass_kernel_spmd as _run

    nc = _bacc.Bacc("TRN2", target_bir_lowering=False, num_devices=1)
    arrays, args = {}, []
    for name in _INS:
        a = _np.ascontiguousarray(inputs[name])
        arrays[f"in_{name}_dram"] = a
        args.append(nc.dram_tensor(f"in_{name}_dram", a.shape, _mybir.dt.from_np(a.dtype), kind="ExternalInput").ap())
    shape = inputs["L0_attn_x"].shape
    experts = inputs["L0_ffn_gate_w"].shape[0]
    fp32 = _mybir.dt.float32
    args.append(nc.dram_tensor("out_0_dram", shape, fp32, kind="ExternalOutput").ap())
    tokens = shape[0] * shape[1] // HALVES
    blocks = -(-(tokens * K // P + experts - 1) // SLOTS) * SLOTS
    for kind, rows in (("xs", (experts + 1) * (tokens + P)), ("ys", blocks * P)):
        args.append([nc.dram_tensor(f"{kind}{h}_dram", (rows, shape[2]), fp32, kind="Internal").ap() for h in range(HALVES)])
    sandwich_kernel(nc, *args)
    r = _run(nc, [arrays], core_ids=[0])
    return r.results[0]["out_0_dram"]
```
